# Optimizing a Trainium2 kernel written in Bass

```python
import numpy as np
import jax
import jax.numpy as jnp

def _softmax(x, axis=-1):
    return jax.nn.softmax(x, axis=axis)

def _gelu(x):
    return jax.nn.gelu(x, approximate=True)

def _silu(x):
    return jax.nn.silu(x)

def _sigmoid(x):
    return jax.nn.sigmoid(x)

def _layernorm(x, axis=-1, eps=1e-05):
    m = jnp.mean(x, axis=axis, keepdims=True)
    v = jnp.var(x, axis=axis, keepdims=True)
    return (x - m) / jnp.sqrt(v + eps)

def _scatter_add(tgt, idx, src, axis=0):
    return tgt.at[idx].add(src)

def _segment_sum(src, seg, n):
    return jax.ops.segment_sum(src, seg, n)
kernel_name = 'mk_prb_d1_jaxref_r8_f8fe02'

def setup_inputs(seed: int=0):
    np.random.seed(seed)
    _w = jnp.asarray

    def _L0_attn_setup():
        import jax, jax.numpy as jnp
        import numpy as np
        B, N, D = (2, 1024, 128)
        H = 16
        HD = D // H
        EPS = 1e-06

        def _feature_map(a):
            return jax.nn.elu(a) + 1.0
        key = jax.random.key(seed)
        ks = jax.random.split(key, 5)
        scale = 1.0 / np.sqrt(D)
        return {'x': jax.random.normal(ks[0], (B, N, D), dtype=jnp.float32), 'Wq': jax.random.normal(ks[1], (D, D), dtype=jnp.float32) * scale, 'Wk': jax.random.normal(ks[2], (D, D), dtype=jnp.float32) * scale, 'Wv': jax.random.normal(ks[3], (D, D), dtype=jnp.float32) * scale, 'Wo': jax.random.normal(ks[4], (D, D), dtype=jnp.float32) * scale}
    _L0_attn_in = _L0_attn_setup()

    def _L0_ffn_setup():
        import jax, jax.numpy as jnp
        import numpy as np
        E, D, F = (8, 128, 512)
        B, S = (4, 256)

        def _layernorm(x, g, b, eps=1e-05):
            mu = jnp.mean(x, axis=-1, keepdims=True)
            var = jnp.var(x, axis=-1, keepdims=True)
            return (x - mu) * jax.lax.rsqrt(var + eps) * g + b
        key = jax.random.key(seed)
        ks = jax.random.split(key, 5)
        return {'input_features': jax.random.normal(ks[0], (B, S, D), jnp.float32), 'centroids': jax.random.normal(ks[1], (E, D), jnp.float32) * 0.1, 'ln_g': jnp.ones((E, D), jnp.float32), 'ln_b': jnp.zeros((E, D), jnp.float32), 'w1': jax.random.normal(ks[2], (E, F, D), jnp.float32) * (1.0 / np.sqrt(D).astype(np.float32)), 'b1': jnp.zeros((E, F), jnp.float32), 'w2': jax.random.normal(ks[3], (E, D, F), jnp.float32) * (1.0 / np.sqrt(F).astype(np.float32)), 'b2': jnp.zeros((E, D), jnp.float32)}
    _L0_ffn_in = _L0_ffn_setup()
    _d = {'L0_attn_x': _L0_attn_in['x'], 'L0_attn_Wq': _L0_attn_in['Wq'], 'L0_attn_Wk': _L0_attn_in['Wk'], 'L0_attn_Wv': _L0_attn_in['Wv'], 'L0_attn_Wo': _L0_attn_in['Wo'], 'L0_ffn_centroids': _L0_ffn_in['centroids'], 'L0_ffn_ln_g': _L0_ffn_in['ln_g'], 'L0_ffn_ln_b': _L0_ffn_in['ln_b'], 'L0_ffn_w1': _L0_ffn_in['w1'], 'L0_ffn_b1': _L0_ffn_in['b1'], 'L0_ffn_w2': _L0_ffn_in['w2'], 'L0_ffn_b2': _L0_ffn_in['b2']}
    _x0 = _d['L0_attn_x']
    _d['L0_attn_x'] = jax.random.normal(jax.random.fold_in(jax.random.key(seed), 1), (16, 256, 128), dtype=_x0.dtype)
    del _x0
    return _d

def reference(L0_attn_x, L0_attn_Wq, L0_attn_Wk, L0_attn_Wv, L0_attn_Wo, L0_ffn_centroids, L0_ffn_ln_g, L0_ffn_ln_b, L0_ffn_w1, L0_ffn_b1, L0_ffn_w2, L0_ffn_b2):

    def _L0_attn_ref(x, Wq, Wk, Wv, Wo):
        import jax, jax.numpy as jnp
        import numpy as np
        B, N, D = (2, 1024, 128)
        H = 16
        HD = D // H
        EPS = 1e-06

        def _feature_map(a):
            return jax.nn.elu(a) + 1.0
        b, n, d = x.shape
        q = _feature_map((x @ Wq.T).reshape(b, n, H, HD))
        k = _feature_map((x @ Wk.T).reshape(b, n, H, HD))
        v = (x @ Wv.T).reshape(b, n, H, HD)
        kv = jnp.einsum('bnhd,bnhm->bhdm', k, v)
        k_sum = k.sum(axis=1)
        numerator = jnp.einsum('bnhd,bhdm->bnhm', q, kv)
        denominator = jnp.einsum('bnhd,bhd->bnh', q, k_sum)[..., None]
        out = numerator / (denominator + EPS)
        out = out.reshape(b, n, d)
        return out @ Wo.T

    def _L0_ffn_ref(input_features, centroids, ln_g, ln_b, w1, b1, w2, b2):
        import jax, jax.numpy as jnp
        import numpy as np
        E, D, F = (8, 128, 512)
        B, S = (4, 256)

        def _layernorm(x, g, b, eps=1e-05):
            mu = jnp.mean(x, axis=-1, keepdims=True)
            var = jnp.var(x, axis=-1, keepdims=True)
            return (x - mu) * jax.lax.rsqrt(var + eps) * g + b
        Bf, Sf, Df = input_features.shape
        x = input_features.reshape(-1, Df)
        aff = x @ centroids.T
        assign = jnp.argmax(aff, axis=1)
        order = jnp.argsort(assign)
        xs = x[order]
        es = assign[order]
        alpha = jax.nn.sigmoid(jnp.take_along_axis(aff[order], es[:, None], axis=1))
        nE = centroids.shape[0]
        y = jnp.zeros_like(xs)
        for e in range(nE):
            h = _layernorm(xs, ln_g[e], ln_b[e])
            h = jax.nn.relu(h @ w1[e].T + b1[e])
            ye = xs + h @ w2[e].T + b2[e]
            y = y + jnp.where((es == e)[:, None], ye, 0.0)
        out_sorted = alpha * y + (1.0 - alpha) * xs
        inv = jnp.argsort(order)
        return out_sorted[inv].reshape(Bf, Sf, Df)
    x = L0_attn_x
    xn = _layernorm(x, axis=-1)
    x = x + _L0_attn_ref(xn, L0_attn_Wq, L0_attn_Wk, L0_attn_Wv, L0_attn_Wo) + _L0_ffn_ref(xn, L0_ffn_centroids, L0_ffn_ln_g, L0_ffn_ln_b, L0_ffn_w1, L0_ffn_b1, L0_ffn_w2, L0_ffn_b2)
    return x

_drawn_inputs = setup_inputs


def setup_inputs(seed=0):
    import zlib

    import numpy as np

    out = dict(_drawn_inputs(seed))
    spreads = {'L0_ffn_ln_g': (1.0, 0.2),
     'L0_ffn_ln_b': (0.0, 0.276),
     'L0_ffn_b1': (0.0, 0.284),
     'L0_ffn_b2': (0.0, 0.1)}
    factors = {'L0_attn_Wq': 7.135, 'L0_attn_Wk': 3.773}
    for name, (base, spread) in spreads.items():
        noise = np.random.default_rng([zlib.crc32(name.encode()), seed]).standard_normal(out[name].shape)
        drawn = base * np.exp(spread * noise) if base else spread * noise
        out[name] = jnp.asarray(drawn.astype(out[name].dtype))
    for name, factor in factors.items():
        out[name] = (out[name] * factor).astype(out[name].dtype)
    return out
```

```python
import concourse.bass as bass
from concourse import mybir
from contextlib import ExitStack


def linear_attention_and_routed_experts(
    nc, x_dram, wq_dram, wk_dram, wv_dram, wo_dram, cent_dram, g_dram, b_dram, w1_dram, b1_dram, w2_dram, b2_dram, out_dram,
):
    f32, bf16, i32 = mybir.dt.float32, mybir.dt.bfloat16, mybir.dt.int32
    ALU = mybir.AluOpType
    ACT = mybir.ActivationFunctionType
    AX = mybir.AxisListType

    P = 128
    NB, NS, D = x_dram.shape
    NTOK = NB * NS
    NT = NTOK // P
    TB = NS // P
    _, FC, E = b1_dram.shape
    F = FC * P
    H = 16
    HD = D // H
    KVW = D + H
    NSLOT = NT + E - 1
    HALF = NB // 2
    EPS_LN, EPS_ATT = 1e-5, 1e-6
    NCH = 4
    TC = NT // NCH
    TG = 4
    NG = NT // TG
    AHEAD = 4
    RING = 12
    PAIRS = (NSLOT - 3) // 2
    POST = 12
    assert D == P and TB == 2 and NSLOT == 2 * PAIRS + 3

    x_t = x_dram.rearrange("b (j p) d -> p (b j) d", p=P)
    out_t = out_dram.rearrange("b (j p) d -> p (b j) d", p=P)
    z_dram = nc.dram_tensor("z_rows", (NTOK, D), f32, kind="Internal").ap()
    y_dram = nc.dram_tensor("y_rows", (NTOK, D), f32, kind="Internal").ap()
    z_t = z_dram.rearrange("(t p) d -> p t d", p=P)
    y_t = y_dram.rearrange("(t p) d -> p t d", p=P)

    ctx = ExitStack()
    with ctx:
        def sb(name, shape, dt=f32):
            return ctx.enter_context(nc.sbuf_tensor(name, shape, dt))

        def sem(name):
            return ctx.enter_context(nc.semaphore(name))

        bank = [ctx.enter_context(nc.psum_tensor(f"bank{i}", [P, 512], f32)) for i in range(8)]

        wq, wk, wv, wo = sb("wq", [P, D]), sb("wk", [P, D]), sb("wv", [P, D]), sb("wo", [P, D])
        cent = sb("cent", [P, E])
        ln_g, ln_b = sb("ln_g", [P, E]), sb("ln_b", [P, E])
        w1 = sb("w1", [P, E * F])
        w2 = sb("w2", [P, E * FC * D])
        b1 = sb("b1", [P, FC, E])
        b2 = sb("b2", [P, E * D])
        ident = sb("ident", [P, P])
        head_mask = sb("head_mask", [P, KVW])
        before = sb("before", [P, P], bf16)
        ones = sb("ones", [P, P], bf16)
        lane = sb("lane", [P, P], bf16)
        rank_e = sb("rank_e", [P, E, NT])
        tile_starts = sb("tile_starts", [P, E, NT])
        slot_no = sb("slot_no", [P, NSLOT + 1])
        tile_no = sb("tile_no", [P, NT])
        part_no1 = sb("part_no1", [P, 1])
        ones_f = sb("ones_f", [P, E * NT])
        x = sb("x", [P, NT, D])
        xn = sb("xn", [P, NT, D])
        z = sb("z", [P, NT, D])
        base = sb("base", [P, NT, D])
        xnT = sb("xnT", [P, NT * P])
        stats = sb("stats", [P, TC, 6])
        mv = sb("mv", [P, NT, 2])
        var_e = sb("var_e", [P, NCH, 2, TC])
        std = sb("std", [P, NCH, 2, TC])
        nw_a, nw_b = sb("nw_a", [P, 2, TC]), sb("nw_b", [P, 2, TC])
        rstd = sb("rstd", [P, NCH, 2, TC])
        rinv = sb("rinv", [P, 2, TC])
        aff = sb("aff", [P, E, NT])
        aff_max = sb("aff_max", [P, NT])
        alpha_e = sb("alpha_e", [P, NT])
        alpha_1 = sb("alpha_1", [P, NT])
        alpha = sb("alpha", [P, NT])
        rt_a, rt_b, rt_c = sb("rt_a", [P, E, NT]), sb("rt_b", [P, E, NT]), sb("rt_c", [P, E, NT])
        first = sb("first", [P, NT])
        chosen = sb("chosen", [P, E, NT], bf16)
        total = sb("total", [P, E, NT])
        upto = sb("upto", [P, E, NT])
        n_e, cnt, last_t, start_t, off = (sb(n, [P, E]) for n in ("n_e", "cnt", "last_t", "start_t", "off"))
        pos = sb("pos", [P, NT])
        pos_i, hi_i, lo_i = sb("pos_i", [P, NT], i32), sb("hi_i", [P, NT], i32), sb("lo_i", [P, NT], i32)
        hi_f, lo_f = sb("hi_f", [P, NT]), sb("lo_f", [P, NT])
        lane_hot = sb("lane_hot", [P, NT, P], bf16)
        slot_hot = sb("slot_hot", [P, NT, NSLOT], bf16)
        slot_val = sb("slot_val", [P, NT, 2, NSLOT], bf16)
        tok_c = sb("tok_c", [P, 2, NSLOT])
        tok_f, tok_neg = sb("tok_f", [P, NSLOT]), sb("tok_neg", [P, NSLOT])
        gather_at, scatter_at = sb("gather_at", [P, NSLOT], i32), sb("scatter_at", [P, NSLOT], i32)
        ex_cmp = sb("ex_cmp", [1, NSLOT + 1, E])
        ex_f, ex_m = sb("ex_f", [1, NSLOT + 1]), sb("ex_m", [1, NSLOT + 1])
        ex_p = [sb(f"ex_p{i}", [1, PAIRS]) for i in range(2)]
        ex_i, ex_pair = sb("ex_i", [1, NSLOT + 1], i32), sb("ex_pair", [1, PAIRS], i32)
        neg_part = sb("neg_part", [P, 2, 4 * P])
        exp_part = sb("exp_part", [P, 2, 4 * P])
        feat = sb("feat", [P, 2, 4 * P])
        v_aug = sb("v_aug", [P, 2, TB, KVW])
        kv_m = sb("kv_m", [P, 2, KVW])
        den, rden = sb("den", [P, TB, H]), sb("rden", [P, TB, H])
        heads = sb("heads", [P, TB, D])
        headsT = sb("headsT", [P, 2, TB * P])
        rows = sb("rows", [P, RING, D])
        y_rows = sb("y_tiles", [P, NSLOT, D])
        zT = sb("zT", [P, 2, P])
        w1_now = sb("w1_now", [P, 2, F])
        hT = sb("hT", [P, 2, F])
        y_back = z

        x_in = [sem(f"x_in{c}") for c in range(NCH)]
        small_in, attw_in, w1_in, w2_in = sem("small_in"), sem("attw_in"), sem("w1_in"), sem("w2_in")
        z_out = sem("z_out")
        gather_in = [sem(f"gather_in{i}") for i in range(AHEAD)]
        y_out = sem("y_out")
        y_in = [sem(f"y_in{c}") for c in range(NCH)]
        out_done = sem("out_done")
        const_step, const_ready, ident_ready = sem("const_step"), sem("const_ready"), sem("ident_ready")
        aug_ready = sem("aug_ready")
        stat_done, mv_done, var_ready, std_ready = sem("stat_done"), sem("mv_done"), sem("var_ready"), sem("std_ready")
        newton, rstd_ready, xn_ready, z_ready = sem("newton"), sem("rstd_ready"), sem("xn_ready"), sem("z_ready")
        base0_ready, xt_done, xnT_ready, aff_done = sem("base0_ready"), sem("xt_done"), sem("xnT_ready"), sem("aff_done")
        route, aff_copied, max_ready, sig_exp, chosen_ready = (
            sem(n) for n in ("route", "aff_copied", "max_ready", "sig_exp", "chosen_ready"))
        alpha_ready, ranks_done, hot_ready, tok_done, index_ready = (
            sem(n) for n in ("alpha_ready", "ranks_done", "hot_ready", "tok_done", "index_ready"))
        expert_ready = sem("expert_ready")
        qk_done, v_done, neg_ready, exp_ready, v_copied, feat_ready = (
            sem(n) for n in ("qk_done", "v_done", "neg_ready", "exp_ready", "v_copied", "feat_ready"))
        kv_done, kvm_ready, num_done, den_ready, rden_ready, heads_ready = (
            sem(n) for n in ("kv_done", "kvm_ready", "num_done", "den_ready", "rden_ready", "heads_ready"))
        ht_done, ht_copied, att_done, base_ready = (sem(n) for n in ("ht_done", "ht_copied", "att_done", "base_ready"))
        gathered, zt_done, zt_ready, w1_ready, ha_done, hd_done, ra_ready, rd_ready, y_done, y_ready = (
            sem(n) for n in ("gathered", "zt_done", "zt_ready", "w1_ready", "ha_done", "hd_done", "ra_ready", "rd_ready", "y_done", "y_ready"))
        scaled, pre_ready, post_ready = sem("scaled"), sem("pre_ready"), sem("post_ready")

        block = ctx.enter_context(nc.Block())

        def wait_for(eng, s, n):
            if not isinstance(n, int) or n > 0:
                eng.wait_ge(s, n)

        def slot(v, j):
            return (v >> (3 * j)) & 7 if j else v & 7

        @block.sync
        def _(sp):
            for c in range(NCH):
                sp.dma_start(x[:, c * TC:(c + 1) * TC, :], x_t[:, c * TC:(c + 1) * TC, :]).then_inc(x_in[c], 16)
            for dst, src in ((cent, cent_dram), (ln_g, g_dram), (ln_b, b_dram)):
                sp.dma_start(dst[:, :], src).then_inc(small_in, 16)
            for dst, src in ((wq, wq_dram), (wk, wk_dram), (wv, wv_dram), (wo, wo_dram)):
                sp.dma_start(dst[:, :], src).then_inc(attw_in, 16)
            for c in range(NCH):
                sp.wait_ge(z_ready, c + 1)
                sp.dma_start(z_t[:, c * TC:(c + 1) * TC, :], z[:, c * TC:(c + 1) * TC, :]).then_inc(z_out, 16)
            sp.dma_start(b1[:, :, :], b1_dram).then_inc(small_in, 16)
            sp.dma_start(b2[:, :], b2_dram.rearrange("e d -> (e d)").partition_broadcast(P)).then_inc(small_in, 16)
            sp.dma_start(w1[:, :], w1_dram).then_inc(w1_in, 16)
            sp.dma_start(w2[:, :], w2_dram).then_inc(w2_in, 16)
            sp.wait_ge(y_out, 16 * NSLOT)
            for c in (3, 0, 1, 2):
                sp.dma_start(y_back[:, c * TC:(c + 1) * TC, :], y_t[:, c * TC:(c + 1) * TC, :]).then_inc(y_in[c], 16)
            for b in range(POST):
                sp.wait_ge(post_ready, b + 1)
                sp.dma_start(out_t[:, TB * b:TB * (b + 1), :], base[:, TB * b:TB * (b + 1), :]).then_inc(out_done, 16)
            for b in range(POST, NB):
                sp.wait_ge(base_ready, b + 1)
                sp.dma_start(out_t[:, TB * b:TB * (b + 1), :], base[:, TB * b:TB * (b + 1), :]).then_inc(out_done, 16)
            sp.wait_ge(out_done, 16 * NB)

        @block.gpsimd
        def _(pool):
            g = nc.gpsimd
            g.memset(ident[:, :], 0.0).then_inc(const_step, 1)
            g.memset(head_mask[:, :], 1.0).then_inc(const_step, 1)
            g.memset(before[:, :], 1.0).then_inc(const_step, 1)
            pool.wait_ge(const_step, 3)
            g.affine_select(out=ident[:, :], in_=ident[:, :], compare_op=ALU.not_equal, fill=1.0, base=0,
                            pattern=[[-1, P]], channel_multiplier=1).then_inc(ident_ready, 1)
            for col, shape in ((head_mask[:, 0:D], [0, HD]), (head_mask[:, D:KVW], [0, 1])):
                pat = [[-HD, H], shape]
                v = col.rearrange("p (h j) -> p h j", h=H)
                g.affine_select(out=v, in_=v, compare_op=ALU.is_ge, fill=0.0, base=0,
                                pattern=pat, channel_multiplier=1).then_inc(const_step, 1)
            pool.wait_ge(const_step, 5)
            for col, shape in ((head_mask[:, 0:D], [0, HD]), (head_mask[:, D:KVW], [0, 1])):
                v = col.rearrange("p (h j) -> p h j", h=H)
                g.affine_select(out=v, in_=v, compare_op=ALU.is_ge, fill=0.0, base=HD - 1,
                                pattern=[[HD, H], shape], channel_multiplier=-1).then_inc(const_ready, 1)
            g.affine_select(out=before[:, :], in_=before[:, :], compare_op=ALU.is_ge, fill=0.0, base=-1,
                            pattern=[[1, P]], channel_multiplier=-1).then_inc(const_ready, 1)
            fine = {"allow_small_or_imprecise_dtypes": True}
            g.iota(lane[:, :], pattern=[[1, P]], base=0, channel_multiplier=0, **fine).then_inc(const_ready, 1)
            g.iota(rank_e[:, :, :], pattern=[[-1, E], [0, NT]], base=E, channel_multiplier=0, **fine).then_inc(const_ready, 1)
            g.iota(tile_starts[:, :, :], pattern=[[0, E], [P, NT]], base=0, channel_multiplier=0, **fine).then_inc(const_ready, 1)
            g.iota(slot_no[:, :], pattern=[[1, NSLOT + 1]], base=0, channel_multiplier=0, **fine).then_inc(const_ready, 1)
            g.iota(tile_no[:, :], pattern=[[1, NT]], base=0, channel_multiplier=0, **fine).then_inc(const_ready, 1)
            g.iota(part_no1[:, :], pattern=[[0, 1]], base=1, channel_multiplier=1, **fine).then_inc(const_ready, 1)
            g.memset(ones[:, :], 1.0).then_inc(const_ready, 1)
            g.memset(ones_f[:, :], 1.0).then_inc(const_ready, 1)
            g.memset(v_aug[:, :, :, D:KVW], 1.0).then_inc(aug_ready, 1)
            for c in range(NCH):
                pool.wait_ge(rstd_ready, c + 1)
                for j in range(TC):
                    t = c * TC + j
                    last = g.tensor_scalar(z[:, t, :], x[:, t, :], mv[:, t, 0:1], rstd[:, c, 1, j:j + 1],
                                           ALU.subtract, ALU.mult)
                last.then_inc(z_ready, 1)
                pool.wait_ge(xn_ready, c + 1)
                g.tensor_tensor(base[:, c * TC:(c + 1) * TC, :], x[:, c * TC:(c + 1) * TC, :],
                                xn[:, c * TC:(c + 1) * TC, :], ALU.add).then_inc(base0_ready, 1)

            def gather(s):
                wait_for(pool, zt_done, s - RING + 1)
                g.indirect_dma_start(
                    out=rows[:, s % RING, :], out_offset=None, in_=z_dram,
                    in_offset=bass.IndirectOffsetOnAxis(ap=gather_at[:, s:s + 1], axis=0),
                ).then_inc(gather_in[s % AHEAD], 16)

            def landed(s):
                pool.wait_ge(gather_in[s % AHEAD], 16 * (s // AHEAD + 1))
                pool.sem_inc(gathered, 1)

            def scatter(s):
                pool.wait_ge(y_ready, s + 1)
                g.indirect_dma_start(
                    out=y_dram, out_offset=bass.IndirectOffsetOnAxis(ap=scatter_at[:, s:s + 1], axis=0),
                    in_=y_rows[:, s, :], in_offset=None, bounds_check=NTOK - 1, oob_is_err=False,
                ).then_inc(y_out, 16)

            pool.wait_ge(z_out, 16 * NCH)
            pool.wait_ge(index_ready, 1)
            for s in range(NSLOT):
                if s >= AHEAD:
                    landed(s - AHEAD)
                gather(s)
                if s >= RING + 1:
                    scatter(s - RING - 1)
            for s in range(NSLOT - AHEAD, NSLOT):
                landed(s)
            for s in range(NSLOT - RING - 1, NSLOT):
                scatter(s)
            pool.wait_ge(alpha_ready, 1)
            n = 0
            for b in (*range(POST, NB), *range(POST)):
                pool.wait_ge(y_in[b * TB // TC], 16)
                for t in range(TB * b, TB * (b + 1)):
                    g.tensor_scalar(y_back[:, t, :], y_back[:, t, :], alpha[:, t:t + 1], None, ALU.mult).then_inc(scaled, 1)
                    n += 1
                pool.wait_ge(scaled, n)
                two = slice(TB * b, TB * (b + 1))
                if b < POST:
                    pool.wait_ge(base_ready, b + 1)
                g.tensor_tensor(base[:, two, :], base[:, two, :], y_back[:, two, :], ALU.add)\
                 .then_inc(post_ready if b < POST else pre_ready, 1)

        @block.scalar
        def _(act):
            a = nc.scalar

            def sqrt_of(c):
                act.wait_ge(var_ready, c + 1)
                a.activation(std[:, c, :, :], var_e[:, c, :, :], ACT.Sqrt).then_inc(std_ready, 1)

            def copy_xnT(gr):
                act.wait_ge(xt_done, gr + 1)
                a.activation(xnT[:, gr * TG * P:(gr + 1) * TG * P], bank[gr % 2][:, :], ACT.Copy).then_inc(xnT_ready, 1)

            sqrt_of(0)
            for c in range(NCH):
                if c + 1 < NCH:
                    sqrt_of(c + 1)
                for gr in range(c * NG // NCH, (c + 1) * NG // NCH):
                    copy_xnT(gr)
            act.wait_ge(max_ready, 1)
            a.activation(alpha_e[:, :], aff_max[:, :], ACT.Exp, scale=-1.0).then_inc(sig_exp, 1)

            def feature_exp(b, par):
                act.wait_ge(qk_done, b + 1)
                a.activation(neg_part[:, par, :], bank[par][:, :], ACT.Relu, scale=-1.0).then_inc(neg_ready, 1)

            def feature_exp2(b, par):
                act.wait_ge(neg_ready, b + 1)
                a.activation(exp_part[:, par, :], neg_part[:, par, :], ACT.Exp, scale=-1.0).then_inc(exp_ready, 1)

            def copy_v(b, par):
                act.wait_ge(v_done, b + 1)
                a.activation(v_aug[:, par, :, 0:D], bank[2][:, 0:TB * D].rearrange("p (j d) -> p j d", j=TB), ACT.Copy)\
                 .then_inc(v_copied, 1)

            def copy_headsT(b, par):
                act.wait_ge(ht_done, b + 1)
                a.activation(headsT[:, par, :], bank[5][:, 0:TB * P], ACT.Copy).then_inc(ht_copied, 1)

            def attention_step(b, par, i):
                if i is None or i < HALF:
                    feature_exp(b, par)
                if i is None or i >= 2:
                    copy_headsT(b - 2, par)
                if i is None or i < HALF:
                    feature_exp2(b, par)
                    copy_v(b, par)

            def attention(b0):
                peeled = 2
                for i in range(peeled):
                    attention_step(b0 + i, i % 2, i)
                with act.Fori(0, (HALF - peeled) // 2) as k:
                    for par in (0, 1):
                        attention_step(k * 2 + (b0 + peeled + par), par, None)
                for i in (HALF, HALF + 1):
                    attention_step(b0 + i, i % 2, i)

            def hidden(s, par, e):
                act.wait_ge(ha_done, s + 1)
                for c in range(FC - 1):
                    last = a.activation(hT[:, par, c * P:(c + 1) * P], bank[2 + par][:, c * P:(c + 1) * P], ACT.Relu,
                                        bias=b1[:, c, bass.ds(e, 1)])
                last.then_inc(ra_ready, 1)

            attention(0)
            act.wait_ge(small_in, 16 * 5)
            act.wait_ge(expert_ready, 2)
            hidden(0, 0, act.value_load(ex_i[0:1, 0:1], min_val=0, max_val=E - 1))
            with act.Fori(0, PAIRS) as k:
                v = act.value_load(ex_pair[0:1, bass.ds(k, 1)], min_val=0, max_val=E ** 4 - 1)
                hidden(k * 2 + 1, 1, slot(v, 1))
                hidden(k * 2 + 2, 0, slot(v, 2))
            for s in (NSLOT - 2, NSLOT - 1):
                hidden(s, s % 2, act.value_load(ex_i[0:1, s:s + 1], min_val=0, max_val=E - 1))
            attention(HALF)

        @block.tensor
        def _(pe):
            t_ = nc.tensor
            pe.wait_ge(ident_ready, 1)
            pe.wait_ge(small_in, 16 * 3)

            def transpose_x(gr):
                pe.wait_ge(xn_ready, gr * TG // TC + 1)
                wait_for(pe, xnT_ready, gr - 1)
                for j in range(TG):
                    last = t_.transpose(bank[gr % 2][:, j * P:(j + 1) * P], xn[:, gr * TG + j, :], ident[:, :])
                last.then_inc(xt_done, 1)

            def affinities(gr):
                pe.wait_ge(xnT_ready, gr + 1)
                for t in range(gr * TG, (gr + 1) * TG):
                    last = t_.matmul(bank[7][:, t * E:(t + 1) * E], xnT[:, t * P:(t + 1) * P], cent[:, :], start=True, stop=True)
                last.then_inc(aff_done, 1)

            for gr in range(NG):
                transpose_x(gr)
                if gr:
                    affinities(gr - 1)
            affinities(NG - 1)

            def num(b, par):
                pe.wait_ge(kvm_ready, b + 1)
                wait_for(pe, heads_ready, b)
                for j in range(TB):
                    last = t_.matmul(bank[4][:, j * KVW:(j + 1) * KVW], feat[:, par, j * P:(j + 1) * P], kv_m[:, par, :],
                                     start=True, stop=True)
                last.then_inc(num_done, 1)

            def turn_heads(b, par):
                pe.wait_ge(heads_ready, b + 1)
                wait_for(pe, ht_copied, b)
                for j in range(TB):
                    last = t_.transpose(bank[5][:, j * P:(j + 1) * P], heads[:, j, :], ident[:, :])
                last.then_inc(ht_done, 1)

            def keys_values(b, par):
                pe.wait_ge(feat_ready, b + 1)
                pe.wait_ge(v_copied, b + 1)
                wait_for(pe, kvm_ready, b)
                for j in range(TB):
                    last = t_.matmul(bank[3][:, 0:KVW], feat[:, par, (TB + j) * P:(TB + j + 1) * P], v_aug[:, par, j, :],
                                     start=(j == 0), stop=(j == TB - 1))
                last.then_inc(kv_done, 1)

            def out_project(b, par):
                pe.wait_ge(ht_copied, b + 1)
                wait_for(pe, base_ready, b)
                for j in range(TB):
                    last = t_.matmul(bank[6][:, j * D:(j + 1) * D], headsT[:, par, j * P:(j + 1) * P], wo[:, :],
                                     start=True, stop=True)
                last.then_inc(att_done, 1)

            def attention_step(b, par, i, b_py):
                if i is None or i >= 2:
                    num(b - 2, par)
                if i is None or i < HALF:
                    batch(b, par, b_py)
                if i is None or i >= 2:
                    turn_heads(b - 2, par)
                if i is None or 1 <= i <= HALF:
                    keys_values(b - 1, 1 - par)
                if i is None or i >= 2:
                    out_project(b - 2, par)

            def batch(b, par, col0):
                wait_for(pe, feat_ready, b - 1)
                cols = [xnT[:, (TB * b + j) * P:(TB * b + j + 1) * P] for j in range(TB)]
                t_.matmul(bank[par][:, 0:TB * P], wq[:, :], xnT[:, TB * b * P:TB * (b + 1) * P], start=True, stop=True)
                for j in range(TB):
                    last = t_.matmul(bank[par][:, (TB + j) * P:(TB + j + 1) * P], cols[j], wk[:, :], start=True, stop=True)
                last.then_inc(qk_done, 1)
                wait_for(pe, v_copied, b)
                for j in range(TB):
                    last = t_.matmul(bank[2][:, j * D:(j + 1) * D], cols[j], wv[:, :], start=True, stop=True)
                last.then_inc(v_done, 1)

            pe.wait_ge(attw_in, 16 * 4)
            pe.wait_ge(aug_ready, 1)
            pe.wait_ge(xnT_ready, NG)
            attention_step(0, 0, 0, 0)

            pe.wait_ge(const_ready, 10)
            pe.wait_ge(chosen_ready, 1)
            pe.wait_ge(aff_copied, 1)
            hot = chosen[:, :, :].rearrange("p e t -> p (e t)")
            t_.matmul(bank[7][:, 0:E * NT], before[:, :], hot, start=True, stop=True)
            t_.matmul(bank[7][:, E * NT:2 * E * NT], ones[:, :], hot, start=True, stop=True).then_inc(ranks_done, 1)
            pe.wait_ge(hot_ready, 1)
            for t in range(NT):
                last = t_.matmul(bank[7][:, 0:2 * NSLOT], lane_hot[:, t, :], slot_val[:, t, :, :].rearrange("p a s -> p (a s)"),
                                 start=(t == 0), stop=(t == NT - 1))
            last.then_inc(tok_done, 1)

            for i in range(1, HALF + 2):
                attention_step(i, i % 2, i, i)

            def turn_rows(s, par, place):
                pe.wait_ge(gathered, s + 1)
                t_.transpose(bank[par][:, 0:P], rows[:, place, :], ident[:, :]).then_inc(zt_done, 1)

            def hidden(s, par):
                pe.wait_ge(zt_ready, s + 1)
                pe.wait_ge(w1_ready, s + 1)
                for c in range(FC):
                    dst = bank[2 + par][:, c * P:(c + 1) * P] if c < FC - 1 else bank[4 + par][:, 0:P]
                    mm = t_.matmul(dst, w1_now[:, par, c * P:(c + 1) * P], zT[:, par, :], start=True, stop=True)
                    if c >= FC - 2:
                        mm.then_inc(ha_done if c == FC - 2 else hd_done, 1)

            def second(s, par, e):
                pe.wait_ge(ra_ready, s + 1)
                pe.wait_ge(rd_ready, s + 1)
                for c in range(FC):
                    last = t_.matmul(bank[6 + par][:, 0:D], hT[:, par, c * P:(c + 1) * P],
                                     w2[:, bass.ds(e * (FC * D) + c * D, D)], start=(c == 0), stop=(c == FC - 1))
                last.then_inc(y_done, 1)

            for s in (feat_ready, v_copied, kvm_ready, heads_ready, ht_copied, base_ready):
                pe.wait_ge(s, HALF)
            pe.wait_ge(index_ready, 1)
            pe.wait_ge(w2_in, 16)
            pe.wait_ge(expert_ready, 2)

            def expert_of(s):
                return pe.value_load(ex_i[0:1, s:s + 1], min_val=0, max_val=E - 1)

            turn_rows(0, 0, 0)
            turn_rows(1, 1, 1)
            hidden(0, 0)
            turn_rows(2, 0, 2)
            hidden(1, 1)
            second(0, 0, expert_of(0))
            with pe.Fori(0, (NSLOT - 3) // RING) as k:
                for n in range(RING // 2):
                    v = pe.value_load(ex_pair[0:1, bass.ds(k * (RING // 2) + n, 1)], min_val=0, max_val=E ** 4 - 1)
                    for j in (0, 1):
                        s, par = k * RING + (2 * n + 2 + j), j
                        turn_rows(s + 1, 1 - par, (2 * n + 3 + j) % RING)
                        hidden(s, par)
                        second(s - 1, 1 - par, slot(v, 1 + j))
            hidden(NSLOT - 1, 0)
            second(NSLOT - 2, 1, expert_of(NSLOT - 2))
            second(NSLOT - 1, 0, expert_of(NSLOT - 1))

            for s in (zt_ready, ra_ready, rd_ready, y_ready):
                pe.wait_ge(s, NSLOT)
            for i in range(HALF + 2):
                attention_step(HALF + i, i % 2, i, HALF + i)

        @block.vector
        def _(dve):
            v_ = nc.vector

            def statistics(c):
                dve.wait_ge(x_in[c], 16)
                if c:
                    dve.wait_ge(mv_done, c)
                for j in range(TC):
                    last = v_.bn_stats(stats[:, j, :], x[:, c * TC + j, :])
                last.then_inc(stat_done, 1)
                dve.wait_ge(stat_done, c + 1)
                for j in range(TC):
                    last = v_.bn_aggr(mv[:, c * TC + j, :], stats[:, j, :])
                last.then_inc(mv_done, 1)
                dve.wait_ge(mv_done, c + 1)
                var = mv[:, c * TC:(c + 1) * TC, 1]
                v_.tensor_scalar(var_e[:, c, 0, :], var, 1.0, EPS_LN, ALU.mult, ALU.add)
                v_.tensor_scalar(var_e[:, c, 1, :], var, 1.0 + EPS_LN, EPS_LN * EPS_LN, ALU.mult, ALU.add).then_inc(var_ready, 1)

            def normalise(c):
                def step(ins, n):
                    ins.then_inc(newton, 1)
                    dve.wait_ge(newton, 4 * c + n)
                dve.wait_ge(std_ready, c + 1)
                dve.wait_ge(var_ready, c + 1)
                step(v_.reciprocal(rinv[:, :, :], std[:, c, :, :]), 1)
                step(v_.tensor_tensor(nw_a[:, :, :], rinv[:, :, :], rinv[:, :, :], ALU.mult), 2)
                step(v_.tensor_tensor(nw_b[:, :, :], nw_a[:, :, :], var_e[:, c, :, :], ALU.mult), 3)
                step(v_.tensor_scalar(nw_a[:, :, :], nw_b[:, :, :], -0.5, 1.5, ALU.mult, ALU.add), 4)
                v_.tensor_tensor(rstd[:, c, :, :], rinv[:, :, :], nw_a[:, :, :], ALU.mult).then_inc(rstd_ready, 1)
                dve.wait_ge(rstd_ready, c + 1)
                for j in range(TC):
                    t = c * TC + j
                    last = v_.tensor_scalar(xn[:, t, :], x[:, t, :], mv[:, t, 0:1], rstd[:, c, 0, j:j + 1], ALU.subtract, ALU.mult)
                last.then_inc(xn_ready, 1)

            statistics(0)
            for c in range(NCH):
                if c + 1 < NCH:
                    statistics(c + 1)
                normalise(c)

            steps = [0]

            def then(ins):
                steps[0] += 1
                ins.then_inc(route, 1)
                dve.wait_ge(route, steps[0])

            def per_e(v):
                return v.unsqueeze(2).to_broadcast([P, E, NT])

            def per_t(v):
                return v.unsqueeze(1).to_broadcast([P, E, NT])

            def t_e(v):
                return v.rearrange("p e t -> p t e")

            dve.wait_ge(aff_done, NG)
            v_.tensor_copy(aff[:, :, :], bank[7][:, 0:NT * E].rearrange("p (t e) -> p e t", e=E)).then_inc(aff_copied, 1)
            dve.wait_ge(aff_copied, 1)
            v_.tensor_reduce(aff_max[:, :], t_e(aff[:, :, :]), AX.X, ALU.max).then_inc(max_ready, 1)
            dve.wait_ge(max_ready, 1)
            dve.wait_ge(const_ready, 10)
            then(v_.tensor_tensor(rt_a[:, :, :], aff[:, :, :], per_t(aff_max[:, :]), ALU.is_equal))
            then(v_.tensor_tensor(rt_b[:, :, :], rt_a[:, :, :], rank_e[:, :, :], ALU.mult))
            then(v_.tensor_reduce(first[:, :], t_e(rt_b[:, :, :]), AX.X, ALU.max))
            v_.tensor_tensor(chosen[:, :, :], rank_e[:, :, :], per_t(first[:, :]), ALU.is_equal).then_inc(chosen_ready, 1)
            dve.wait_ge(sig_exp, 1)
            then(v_.tensor_scalar(alpha_1[:, :], alpha_e[:, :], 1.0, None, ALU.add))
            v_.reciprocal(alpha[:, :], alpha_1[:, :]).then_inc(alpha_ready, 1)
            dve.wait_ge(ranks_done, 1)
            rank_p = bank[7][:, 0:E * NT].rearrange("p (e t) -> p e t", e=E)
            total_p = bank[7][:, E * NT:2 * E * NT].rearrange("p (e t) -> p e t", e=E)
            then(v_.tensor_copy(total[:, :, :], total_p))
            flat = [v[:, :, :].rearrange("p e t -> p (e t)") for v in (total, upto)]
            then(v_.tensor_tensor_scan(flat[1], ones_f[:, :], flat[0], 0.0, ALU.mult, ALU.add))
            then(v_.tensor_tensor(rt_a[:, :, :], upto[:, :, :], total[:, :, :], ALU.subtract))
            then(v_.tensor_tensor(n_e[:, :], upto[:, :, NT - 1], rt_a[:, :, 0], ALU.subtract))
            then(v_.tensor_tensor(rt_b[:, :, :], per_e(n_e[:, :]), tile_starts[:, :, :], ALU.is_gt))
            then(v_.tensor_reduce(cnt[:, :], rt_b[:, :, :], AX.X, ALU.add))
            then(v_.tensor_tensor_scan(last_t[:, :], ones_f[:, 0:E], cnt[:, :], 0.0, ALU.mult, ALU.add))
            then(v_.tensor_tensor(start_t[:, :], last_t[:, :], cnt[:, :], ALU.subtract))
            then(v_.scalar_tensor_tensor(off[:, :], start_t[:, :], float(P), rt_a[:, :, 0], ALU.mult, ALU.subtract))
            then(v_.tensor_tensor(rt_b[:, :, :], rt_a[:, :, :], rank_p, ALU.add))
            then(v_.tensor_tensor(rt_c[:, :, :], rt_b[:, :, :], per_e(off[:, :]), ALU.add))
            then(v_.tensor_tensor(rt_a[:, :, :], rt_c[:, :, :], chosen[:, :, :], ALU.mult))
            then(v_.tensor_reduce(pos[:, :], t_e(rt_a[:, :, :]), AX.X, ALU.add))
            then(v_.tensor_copy(pos_i[:, :], pos[:, :]))
            v_.tensor_scalar(hi_i[:, :], pos_i[:, :], 7, None, ALU.arith_shift_right)
            then(v_.tensor_scalar(lo_i[:, :], pos_i[:, :], P - 1, None, ALU.bitwise_and))
            v_.tensor_copy(hi_f[:, :], hi_i[:, :])
            then(v_.tensor_copy(lo_f[:, :], lo_i[:, :]))
            for t in range(NT):
                v_.tensor_scalar(lane_hot[:, t, :], lane[:, :], lo_f[:, t:t + 1], None, ALU.is_equal)
            then(v_.tensor_tensor(slot_hot[:, :, :], slot_no[:, 0:NSLOT].unsqueeze(1).to_broadcast([P, NT, NSLOT]),
                                  hi_f[:, :].unsqueeze(2).to_broadcast([P, NT, NSLOT]), ALU.is_equal))
            v_.tensor_scalar(slot_val[:, :, 0, :], slot_hot[:, :, :], part_no1[:, :], None, ALU.mult)
            v_.tensor_tensor(slot_val[:, :, 1, :], slot_hot[:, :, :], tile_no[:, :].unsqueeze(2).to_broadcast([P, NT, NSLOT]),
                             ALU.mult).then_inc(hot_ready, 1)
            then(v_.tensor_tensor(ex_cmp[:, :, :], slot_no[0:1, :].unsqueeze(2).to_broadcast([1, NSLOT + 1, E]),
                                  last_t[0:1, :].unsqueeze(1).to_broadcast([1, NSLOT + 1, E]), ALU.is_ge))
            then(v_.tensor_reduce(ex_f[:, :], ex_cmp[:, :, :], AX.X, ALU.add))
            then(v_.tensor_scalar(ex_m[:, :], ex_f[:, :], float(E - 1), None, ALU.min))
            v_.tensor_copy(ex_i[:, :], ex_m[:, :]).then_inc(expert_ready, 1)
            ev = [ex_m[:, j:j + 2 * PAIRS - 1:2] for j in range(4)]
            then(v_.scalar_tensor_tensor(ex_p[0][:, :], ev[3], float(E), ev[2], ALU.mult, ALU.add))
            then(v_.scalar_tensor_tensor(ex_p[1][:, :], ex_p[0][:, :], float(E), ev[1], ALU.mult, ALU.add))
            v_.scalar_tensor_tensor(ex_pair[:, :], ex_p[1][:, :], float(E), ev[0], ALU.mult, ALU.add).then_inc(expert_ready, 1)
            dve.wait_ge(tok_done, 1)
            then(v_.tensor_copy(tok_c[:, :, :], bank[7][:, 0:2 * NSLOT].rearrange("p (a s) -> p a s", a=2)))
            then(v_.scalar_tensor_tensor(tok_f[:, :], tok_c[:, 1, :], float(P), tok_c[:, 0, :], ALU.mult, ALU.add))
            v_.tensor_scalar(gather_at[:, :], tok_f[:, :], -1.0, 0.0, ALU.add, ALU.max)
            then(v_.tensor_scalar(tok_neg[:, :], tok_f[:, :], 0.5, float(2 * NTOK), ALU.is_lt, ALU.mult))
            v_.scalar_tensor_tensor(scatter_at[:, :], tok_f[:, :], -1.0, tok_neg[:, :], ALU.add, ALU.add).then_inc(index_ready, 1)

            def divide(b, par):
                dve.wait_ge(num_done, b + 1)
                nd = bank[4][:, 0:TB * KVW].rearrange("p (j c) -> p j c", j=TB)
                v_.tensor_scalar(den[:, :, :], nd[:, :, D:KVW], EPS_ATT, None, ALU.add).then_inc(den_ready, 1)
                dve.wait_ge(den_ready, b + 1)
                v_.reciprocal(rden[:, :, :], den[:, :, :]).then_inc(rden_ready, 1)
                dve.wait_ge(rden_ready, b + 1)
                wait_for(dve, ht_done, b)
                for j in range(TB):
                    last = v_.tensor_tensor(heads[:, j, :].rearrange("p (h m) -> p h m", h=H),
                                            nd[:, j, 0:D].rearrange("p (h m) -> p h m", h=H),
                                            rden[:, j, :].unsqueeze(2).to_broadcast([P, H, HD]), ALU.mult)
                last.then_inc(heads_ready, 1)

            def features(b, par):
                dve.wait_ge(exp_ready, b + 1)
                wait_for(dve, num_done, b - 1)
                v_.scalar_tensor_tensor(feat[:, par, :], bank[par][:, :], 0.0, exp_part[:, par, :], ALU.max, ALU.add)\
                  .then_inc(feat_ready, 1)

            def mask_kv(b, par):
                dve.wait_ge(kv_done, b + 1)
                v_.tensor_tensor(kv_m[:, par, :], bank[3][:, 0:KVW], head_mask[:, :], ALU.mult).then_inc(kvm_ready, 1)

            def add_attention(b, par):
                dve.wait_ge(att_done, b + 1)
                if isinstance(b, int) and b >= POST:
                    dve.wait_ge(pre_ready, b - POST + 1)
                two = base[:, TB * b:TB * (b + 1), :] if isinstance(b, int) else base[:, bass.ds(b * TB, TB), :]
                v_.tensor_tensor(two, bank[6][:, 0:TB * D].rearrange("p (j d) -> p j d", j=TB), two, ALU.add).then_inc(base_ready, 1)

            def attention_step(b, par, i):
                if i is None or i >= 2:
                    divide(b - 2, par)
                if i is None or 1 <= i <= HALF:
                    features(b - 1, 1 - par)
                    mask_kv(b - 1, 1 - par)
                if i is None or i >= 2:
                    add_attention(b - 2, par)

            def turned(s, par, e):
                dve.wait_ge(zt_done, s + 1)
                v_.tensor_scalar(zT[:, par, :], bank[par][:, 0:P], ln_g[:, bass.ds(e, 1)], ln_b[:, bass.ds(e, 1)],
                                 ALU.mult, ALU.add).then_inc(zt_ready, 1)
                v_.tensor_copy(w1_now[:, par, :], w1[:, bass.ds(e * F, F)]).then_inc(w1_ready, 1)

            def hidden(s, par, e):
                dve.wait_ge(hd_done, s + 1)
                v_.tensor_scalar(hT[:, par, (FC - 1) * P:F], bank[4 + par][:, 0:P], b1[:, FC - 1, bass.ds(e, 1)], 0.0,
                                 ALU.add, ALU.max).then_inc(rd_ready, 1)

            def result(s, par, e):
                dve.wait_ge(y_done, s + 1)
                dst = y_rows[:, s, :] if isinstance(s, int) else y_rows[:, bass.ds(s, 1), :].rearrange("p s d -> p (s d)")
                v_.tensor_tensor(dst, bank[6 + par][:, 0:D], b2[:, bass.ds(e * D, D)], ALU.add).then_inc(y_ready, 1)

            dve.wait_ge(base0_ready, NCH)
            for i in range(HALF + 2):
                attention_step(i, i % 2, i)

            def expert_of(s):
                return dve.value_load(ex_i[0:1, s:s + 1], min_val=0, max_val=E - 1)

            dve.wait_ge(expert_ready, 2)
            dve.wait_ge(small_in, 16 * 5)
            dve.wait_ge(w1_in, 16)
            e0, e1 = expert_of(0), expert_of(1)
            turned(0, 0, e0)
            turned(1, 1, e1)
            hidden(0, 0, e0)
            with dve.Fori(0, PAIRS) as k:
                v = dve.value_load(ex_pair[0:1, bass.ds(k, 1)], min_val=0, max_val=E ** 4 - 1)
                for n, (s, par) in enumerate(((k * 2 + 1, 1), (k * 2 + 2, 0))):
                    turned(s + 1, 1 - par, slot(v, n + 2))
                    hidden(s, par, slot(v, n + 1))
                    result(s - 1, 1 - par, slot(v, n))
            for s in (NSLOT - 2, NSLOT - 1):
                if s + 1 < NSLOT:
                    turned(s + 1, (s + 1) % 2, expert_of(s + 1))
                hidden(s, s % 2, expert_of(s))
                result(s - 1, (s - 1) % 2, expert_of(s - 1))
            result(NSLOT - 1, (NSLOT - 1) % 2, expert_of(NSLOT - 1))
            for i in range(HALF + 2):
                attention_step(HALF + i, i % 2, i)


def kernel(L0_attn_x, L0_attn_Wq, L0_attn_Wk, L0_attn_Wv, L0_attn_Wo, L0_ffn_centroids, L0_ffn_ln_g, L0_ffn_ln_b,
           L0_ffn_w1, L0_ffn_b1, L0_ffn_w2, L0_ffn_b2):
    import numpy as np
    import concourse.bacc as bacc
    from concourse.bass_utils import run_bass_kernel_spmd

    P = 128
    x = np.ascontiguousarray(L0_attn_x)
    w1, b1, w2 = (np.asarray(v) for v in (L0_ffn_w1, L0_ffn_b1, L0_ffn_w2))
    E, F, D = w1.shape
    C = F // P
    laid = {
        "x": x,
        "wqT": np.asarray(L0_attn_Wq).T, "wkT": np.asarray(L0_attn_Wk).T,
        "wvT": np.asarray(L0_attn_Wv).T, "woT": np.asarray(L0_attn_Wo).T,
        "centT": np.asarray(L0_ffn_centroids).T, "gT": np.asarray(L0_ffn_ln_g).T, "bT": np.asarray(L0_ffn_ln_b).T,
        "w1T": w1.transpose(2, 0, 1).reshape(D, E * F),
        "b1T": b1.reshape(E, C, P).transpose(2, 1, 0),
        "w2T": w2.reshape(E, D, C, P).transpose(3, 0, 2, 1).reshape(P, E * C * D),
        "b2": np.asarray(L0_ffn_b2),
    }
    nc = bacc.Bacc("TRN2", target_bir_lowering=False, num_devices=1)
    arrays, args = {}, []
    for name, a in laid.items():
        a = np.ascontiguousarray(a)
        arrays["in_" + name] = a
        args.append(nc.dram_tensor("in_" + name, a.shape, mybir.dt.from_np(a.dtype), kind="ExternalInput").ap())
    args.append(nc.dram_tensor("out", x.shape, mybir.dt.from_np(x.dtype), kind="ExternalOutput").ap())
    linear_attention_and_routed_experts(nc, *args)
    r = run_bass_kernel_spmd(nc, [arrays], core_ids=[0])
    return r.results[0]["out"]
```

```python
import concourse.bass as bass
from concourse import mybir
from contextlib import ExitStack


def linear_attention_and_routed_experts(
    nc, x_dram, wq_dram, wk_dram, wv_dram, wo_dram, cent_dram, g_dram, b_dram, w1_dram, b1_dram, w2_dram, b2_dram, out_dram,
):
    f32, bf16, i32 = mybir.dt.float32, mybir.dt.bfloat16, mybir.dt.int32
    ALU = mybir.AluOpType
    ACT = mybir.ActivationFunctionType
    AX = mybir.AxisListType

    P = 128
    NB, NS, D = x_dram.shape
    NTOK = NB * NS
    NT = NTOK // P
    TB = NS // P
    _, FC, E = b1_dram.shape
    F = FC * P
    H = 16
    HD = D // H
    KVW = D + H
    NSLOT = NT + E - 1
    TPB = 3
    EPS_LN, EPS_ATT = 1e-5, 1e-6
    NCH = 4
    TC = NT // NCH
    TG = 4
    LAG = 2
    XN_ACT = 2
    NG = NT // TG
    AHEAD = 4
    RING = 12
    PAIRS = (NSLOT - 3) // 2
    TURNS = 2 * PAIRS // RING
    NB1 = 2 * PAIRS // TPB
    KV_LAG = 2
    RANKS_AT, TOKENS_AT, PART_AT, TILE_AT = 2, 11, 8, 8
    WORD = 5
    LANES_PIECE = 8
    POOL_ADDS = 7
    DVE_ADDS = {5: (7, 8), 6: (9, 10, 11, 12, 13, 14, 15)}
    Y_ORDER = (0, 1, 2, 3)
    OUT_ORDER = (0, 7, 1, 8, 2, 9, 3, 10, 4, 11, 5, 12, 6, 13, 14, 15)
    assert D == P and TB == 2 and NSLOT == 2 * PAIRS + 3 and 2 * PAIRS == TURNS * RING and RING % (2 * TPB) == 0

    x_t = x_dram.rearrange("b (j p) d -> p (b j) d", p=P)
    out_t = out_dram.rearrange("b (j p) d -> p (b j) d", p=P)
    z_dram = nc.dram_tensor("z_rows", (NTOK, D), f32, kind="Internal").ap()
    y_dram = nc.dram_tensor("y_rows", (NTOK, D), f32, kind="Internal").ap()
    z_t = z_dram.rearrange("(t p) d -> p t d", p=P)
    y_t = y_dram.rearrange("(t p) d -> p t d", p=P)

    ctx = ExitStack()
    with ctx:
        def sb(name, shape, dt=f32):
            return ctx.enter_context(nc.sbuf_tensor(name, shape, dt))

        def sem(name):
            return ctx.enter_context(nc.semaphore(name))

        bank = [ctx.enter_context(nc.psum_tensor(f"bank{i}", [P, 512], f32)) for i in range(8)]

        wq, wk, wo = sb("wq", [P, D]), sb("wk", [P, D]), sb("wo", [P, D])
        cent_wv = sb("cent_wv", [P, E + D])
        ln_g, ln_b = sb("ln_g", [P, E]), sb("ln_b", [P, E])
        w1 = sb("w1", [P, E * F])
        w2 = sb("w2", [P, E * FC * D])
        b1 = sb("b1", [P, FC, E])
        b2 = sb("b2", [P, E * D])
        ident = sb("ident", [P, P])
        head_mask = sb("head_mask", [P, KVW])
        before = sb("before", [P, P], bf16)
        ones = sb("ones", [P, P], bf16)
        lane = sb("lane", [P, P], bf16)
        rank_e = sb("rank_e", [P, E, NT])
        tile_starts = sb("tile_starts", [P, E, NT])
        slot_no = sb("slot_no", [P, NSLOT + 1])
        tile_no = sb("tile_no", [P, NT])
        part_no1 = sb("part_no1", [P, 1])
        ones_f = sb("ones_f", [P, E * NT])
        x = sb("x", [P, NT, D])
        xn_y = sb("xn_and_y_tiles", [P, NSLOT, D])
        xn = xn_y[:, 0:NT, :]
        z = sb("z", [P, NT, D])
        base = sb("base", [P, NT, D])
        xnT = sb("xnT", [P, NT * P])
        stats = sb("stats", [P, 2, TC, 6])
        ms_a, ms_b = sb("ms_a", [P, 3, TC]), sb("ms_b", [P, 2, TC])
        mean = sb("mean", [P, NT])
        shift = sb("shift", [P, NT])
        zscale = sb("zscale", [P, NT])
        nw_c = sb("nw_c", [P, TC])
        var_e = sb("var_e", [P, NCH, 2, TC])
        std = sb("std", [P, NCH, 2, TC])
        nw_a, nw_b = sb("nw_a", [P, 2, TC]), sb("nw_b", [P, 2, TC])
        rstd = sb("rstd", [P, NCH, 2, TC])
        rinv = sb("rinv", [P, 2, TC])
        aff_max = sb("aff_max", [P, NT])
        alpha_e = sb("alpha_e", [P, NT])
        alpha_1 = sb("alpha_1", [P, NT])
        alpha = sb("alpha", [P, NT])
        rt_a, rt_b, rt_c = sb("rt_a", [P, E, NT]), sb("rt_b", [P, E, NT]), sb("rt_c", [P, E, NT])
        first = sb("first", [P, NT])
        chosen = sb("chosen", [P, E, NT], bf16)
        total = sb("total", [P, E, NT])
        upto = sb("upto", [P, E, NT])
        n_e, cnt, last_t, start_t, off = (sb(n, [P, E]) for n in ("n_e", "cnt", "last_t", "start_t", "off"))
        pos = sb("pos", [P, NT])
        pos_i, hi_i, lo_i = sb("pos_i", [P, NT], i32), sb("hi_i", [P, NT], i32), sb("lo_i", [P, NT], i32)
        hi_f, lo_f = sb("hi_f", [P, NT]), sb("lo_f", [P, NT])
        lane_hot = sb("lane_hot", [P, NT, P], bf16)
        slot_hot = sb("slot_hot", [P, NT, NSLOT], bf16)
        slot_val = sb("slot_val", [P, NT, 2, NSLOT], bf16)
        tok_c = sb("tok_c", [P, 2, NSLOT])
        tok_f, tok_neg = sb("tok_f", [P, NSLOT]), sb("tok_neg", [P, NSLOT])
        gather_at, scatter_at = sb("gather_at", [P, NSLOT], i32), sb("scatter_at", [P, NSLOT], i32)
        ex_cmp = sb("ex_cmp", [1, NSLOT + 1, E])
        ex_f, ex_m = sb("ex_f", [1, NSLOT + 1]), sb("ex_m", [1, NSLOT + 1])
        ex_p = [sb(f"ex_p{i}", [1, PAIRS]) for i in range(2)]
        ex_i, ex_pair = sb("ex_i", [1, NSLOT + 1], i32), sb("ex_pair", [1, PAIRS], i32)
        v_all = sb("v_all", [P, NT, E + KVW])
        feat_k = x
        kv_m = sb("kv_m", [P, NB, KVW])
        k_neg, k_pos, k_exp = (sb(n, [P, 2, TB * P]) for n in ("k_neg", "k_pos", "k_exp"))
        kv_c = sb("kv_c", [P, 2, KVW])
        q_neg, q_exp, feat_q = k_neg, k_exp, k_pos
        den, rden = sb("den", [P, TB, H]), sb("rden", [P, TB, H])
        heads = sb("heads", [P, TB, D])
        headsT = sb("headsT", [P, 2, TB * P])
        rows = sb("rows", [P, RING, D])
        y_rows = xn_y
        zT = sb("zT", [P, 2, P])
        w1_now = sb("w1_now", [P, 2, F])
        hT = sb("hT", [P, 2, F])
        y_back = z

        x_in = [sem(f"x_in{c}") for c in range(NCH)]
        cent_wv_in, small_in, bias_in, attw_in, w1_in, w2_in = sem("cent_wv_in"), sem("small_in"), sem("bias_in"), sem("attw_in"), sem("w1_in"), sem("w2_in")
        z_out = sem("z_out")
        gather_in = [sem(f"gather_in{i}") for i in range(AHEAD)]
        y_out = sem("y_out")
        y_in = [sem(f"y_in{c}") for c in range(NCH)]
        out_done = sem("out_done")
        const_step, const_ready, ident_ready = sem("const_step"), sem("const_ready"), sem("ident_ready")
        aug_ready = sem("aug_ready")
        stat_done, chain, var_ready, std_ready = sem("stat_done"), sem("chain"), sem("var_ready"), sem("std_ready")
        xn_by_dve, xn_by_act, z_ready = sem("xn_by_dve"), sem("xn_by_act"), sem("z_ready")
        rstd_ready = sem("rstd_ready")
        zscale_ready = sem("zscale_ready")
        xt_done, xnT_ready = sem("xt_done"), sem("xnT_ready")
        route, max_ready, sig_exp, chosen_ready = (sem(n) for n in ("route", "max_ready", "sig_exp", "chosen_ready"))
        alpha_ready, ranks_done, tok_done, index_ready, expert_ready = (
            sem(n) for n in ("alpha_ready", "ranks_done", "tok_done", "index_ready", "expert_ready"))
        lane_ready, slot_hot_ready, part_val_ready, tile_val_ready = (
            sem(n) for n in ("lane_ready", "slot_hot_ready", "part_val_ready", "tile_val_ready"))
        v_done, v_copied = sem("v_done"), sem("v_copied")
        k_done, k_neg_ready, k_read, k_exp_ready, k_ready, kv_done, kv_copied, kvm_ready = (
            sem(n) for n in ("k_done", "k_neg_ready", "k_read", "k_exp_ready", "k_ready", "kv_done", "kv_copied", "kvm_ready"))
        q_done, q_neg_ready, q_exp_ready, q_ready = (sem(n) for n in ("q_done", "q_neg_ready", "q_exp_ready", "q_ready"))
        num_done, den_ready, rden_ready, heads_ready = (sem(n) for n in ("num_done", "den_ready", "rden_ready", "heads_ready"))
        ht_done, ht_copied, att_done = (sem(n) for n in ("ht_done", "ht_copied", "att_done"))
        base_ready = sem("base_ready")
        gathered, zt_done, zt_ready, w1_ready, h_done, h_ready, y_done, y_ready = (
            sem(n) for n in ("gathered", "zt_done", "zt_ready", "w1_ready", "h_done", "h_ready", "y_done", "y_ready"))
        scaled, pool_added, dve_added = sem("scaled"), sem("pool_added"), sem("dve_added")

        block = ctx.enter_context(nc.Block())

        Q, NUM, HT, OUT = range(4)

        def bank_of(stage, par, last):
            return bank[((par, 4 - par, 5, 2) if last else (5, 4, 5, 4))[stage]]

        def wait_for(eng, s, n):
            if not isinstance(n, int) or n > 0:
                eng.wait_ge(s, n)

        def some(v, first, n):
            return v[:, first:first + n] if isinstance(first, int) else v[:, bass.ds(first, n)]

        def slot(v, j):
            return (v >> (3 * j)) & 7 if j else v & 7

        @block.sync
        def _(sp):
            for c in range(NCH):
                sp.dma_start(x[:, c * TC:(c + 1) * TC, :], x_t[:, c * TC:(c + 1) * TC, :]).then_inc(x_in[c], 16)
                if c == 0:
                    sp.dma_start(cent_wv[:, 0:E], cent_dram).then_inc(cent_wv_in, 16)
                    sp.dma_start(cent_wv[:, E:E + D], wv_dram).then_inc(cent_wv_in, 16)
            for dst, src in ((ln_g, g_dram), (ln_b, b_dram)):
                sp.dma_start(dst[:, :], src).then_inc(small_in, 16)
            for dst, src in ((wq, wq_dram), (wk, wk_dram), (wo, wo_dram)):
                sp.dma_start(dst[:, :], src).then_inc(attw_in, 16)
            sp.dma_start(b1[:, :, :], b1_dram).then_inc(bias_in, 16)
            sp.dma_start(b2[:, :], b2_dram.rearrange("e d -> (e d)").partition_broadcast(P)).then_inc(bias_in, 16)
            sp.dma_start(w1[:, :], w1_dram).then_inc(w1_in, 16)
            for c in range(NCH):
                sp.wait_ge(z_ready, c + 1)
                sp.dma_start(z_t[:, c * TC:(c + 1) * TC, :], z[:, c * TC:(c + 1) * TC, :]).then_inc(z_out, 16)
            sp.dma_start(w2[:, :], w2_dram).then_inc(w2_in, 16)
            sp.wait_ge(y_out, 16 * NSLOT)
            for c in Y_ORDER:
                sp.dma_start(y_back[:, c * TC:(c + 1) * TC, :], y_t[:, c * TC:(c + 1) * TC, :]).then_inc(y_in[c], 16)
            by_pool = by_dve = 0
            for b in OUT_ORDER:
                if b < POOL_ADDS:
                    by_pool += 1
                    sp.wait_ge(pool_added, by_pool)
                else:
                    by_dve += 1
                    sp.wait_ge(dve_added, by_dve)
                sp.dma_start(out_t[:, TB * b:TB * (b + 1), :], base[:, TB * b:TB * (b + 1), :]).then_inc(out_done, 16)
            sp.wait_ge(out_done, 16 * NB)

        @block.gpsimd
        def _(pool):
            g = nc.gpsimd
            g.memset(ident[:, :], 0.0).then_inc(const_step, 1)
            g.memset(head_mask[:, :], 1.0).then_inc(const_step, 1)
            g.memset(before[:, :], 1.0).then_inc(const_step, 1)
            pool.wait_ge(const_step, 3)
            g.affine_select(out=ident[:, :], in_=ident[:, :], compare_op=ALU.not_equal, fill=1.0, base=0,
                            pattern=[[-1, P]], channel_multiplier=1).then_inc(ident_ready, 1)
            for col, shape in ((head_mask[:, 0:D], [0, HD]), (head_mask[:, D:KVW], [0, 1])):
                pat = [[-HD, H], shape]
                v = col.rearrange("p (h j) -> p h j", h=H)
                g.affine_select(out=v, in_=v, compare_op=ALU.is_ge, fill=0.0, base=0,
                                pattern=pat, channel_multiplier=1).then_inc(const_step, 1)
            pool.wait_ge(const_step, 5)
            for col, shape in ((head_mask[:, 0:D], [0, HD]), (head_mask[:, D:KVW], [0, 1])):
                v = col.rearrange("p (h j) -> p h j", h=H)
                g.affine_select(out=v, in_=v, compare_op=ALU.is_ge, fill=0.0, base=HD - 1,
                                pattern=[[HD, H], shape], channel_multiplier=-1).then_inc(const_ready, 1)
            g.affine_select(out=before[:, :], in_=before[:, :], compare_op=ALU.is_ge, fill=0.0, base=-1,
                            pattern=[[1, P]], channel_multiplier=-1).then_inc(const_ready, 1)
            fine = {"allow_small_or_imprecise_dtypes": True}
            g.iota(lane[:, :], pattern=[[1, P]], base=0, channel_multiplier=0, **fine).then_inc(const_ready, 1)
            g.iota(rank_e[:, :, :], pattern=[[-1, E], [0, NT]], base=E, channel_multiplier=0, **fine).then_inc(const_ready, 1)
            g.iota(tile_starts[:, :, :], pattern=[[0, E], [P, NT]], base=0, channel_multiplier=0, **fine).then_inc(const_ready, 1)
            g.iota(slot_no[:, :], pattern=[[1, NSLOT + 1]], base=0, channel_multiplier=0, **fine).then_inc(const_ready, 1)
            g.iota(tile_no[:, :], pattern=[[1, NT]], base=0, channel_multiplier=0, **fine).then_inc(const_ready, 1)
            g.iota(part_no1[:, :], pattern=[[0, 1]], base=1, channel_multiplier=1, **fine).then_inc(const_ready, 1)
            g.memset(ones[:, :], 1.0).then_inc(const_ready, 1)
            g.memset(ones_f[:, :], 1.0).then_inc(const_ready, 1)
            g.memset(v_all[:, :, E + D:E + KVW], 1.0).then_inc(aug_ready, 1)
            for c in range(NCH):
                part = slice(c * TC, (c + 1) * TC)
                pool.wait_ge(zscale_ready, c + 1)
                pool.wait_ge(xn_by_dve, (c + 1) * TC // TG)
                pool.wait_ge(xn_by_act, (c + 1) * TC // TG)
                g.tensor_tensor(z[:, part, :], xn[:, part, :], zscale[:, part].unsqueeze(2).to_broadcast([P, TC, D]),
                                ALU.mult).then_inc(z_ready, 1)
                add = g.tensor_tensor(base[:, part, :], x[:, part, :], xn[:, part, :], ALU.add)
            add.then_inc(base_ready, 1)

            def tile_values():
                pool.wait_ge(slot_hot_ready, 1)
                g.tensor_tensor(slot_val[:, :, 1, :], slot_hot[:, :, :], tile_no[:, :].unsqueeze(2).to_broadcast([P, NT, NSLOT]),
                                ALU.mult).then_inc(tile_val_ready, 1)

            def features_k(b, par):
                pool.wait_ge(k_exp_ready, b + 1)
                g.tensor_tensor(feat_k[:, TB * b:TB * (b + 1), :].rearrange("p j d -> p (j d)"), k_pos[:, par, :], k_exp[:, par, :],
                                ALU.add).then_inc(k_ready, 1)

            def mask_kv(b, par):
                pool.wait_ge(kv_copied, b + 1)
                g.tensor_tensor(kv_m[:, b, :], kv_c[:, par, :], head_mask[:, :], ALU.mult).then_inc(kvm_ready, 1)

            pool.wait_ge(base_ready, 1)
            for i in range(NB + KV_LAG + 1):
                if i == TILE_AT:
                    tile_values()
                if i < NB:
                    features_k(i, i % 2)
                if i > KV_LAG:
                    mask_kv(i - KV_LAG - 1, (i - KV_LAG - 1) % 2)

            def gather(s):
                wait_for(pool, zt_done, s - RING + 1)
                g.indirect_dma_start(
                    out=rows[:, s % RING, :], out_offset=None, in_=z_dram,
                    in_offset=bass.IndirectOffsetOnAxis(ap=gather_at[:, s:s + 1], axis=0),
                ).then_inc(gather_in[s % AHEAD], 16)

            def landed(s):
                pool.wait_ge(gather_in[s % AHEAD], 16 * (s // AHEAD + 1))
                pool.sem_inc(gathered, 1)

            def scatter(s):
                pool.wait_ge(y_ready, s + 1)
                g.indirect_dma_start(
                    out=y_dram, out_offset=bass.IndirectOffsetOnAxis(ap=scatter_at[:, s:s + 1], axis=0),
                    in_=y_rows[:, s, :], in_offset=None, bounds_check=NTOK - 1, oob_is_err=False,
                ).then_inc(y_out, 16)

            pool.wait_ge(z_out, 16 * NCH)
            pool.wait_ge(index_ready, 1)
            sent = 0
            for s in range(NSLOT):
                if s >= AHEAD:
                    landed(s - AHEAD)
                gather(s)
                if s > RING and s % 3:
                    scatter(sent)
                    sent += 1
            for s in range(NSLOT - AHEAD, NSLOT):
                landed(s)
            for s in range(sent, NSLOT):
                scatter(s)
            pool.wait_ge(alpha_ready, 1)
            pool.wait_ge(base_ready, POOL_ADDS + 1)
            for b in range(POOL_ADDS):
                pool.wait_ge(y_in[b * TB // TC], 16)
                two = slice(TB * b, TB * (b + 1))
                g.tensor_tensor(y_back[:, two, :], y_back[:, two, :], alpha[:, two].unsqueeze(2).to_broadcast([P, TB, D]),
                                ALU.mult).then_inc(scaled, 1)
                pool.wait_ge(scaled, b + 1)
                g.tensor_tensor(base[:, two, :], base[:, two, :], y_back[:, two, :], ALU.add).then_inc(pool_added, 1)

        @block.scalar
        def _(act):
            a = nc.scalar

            def sqrt_of(c):
                act.wait_ge(var_ready, c + 1)
                a.activation(std[:, c, :, :], var_e[:, c, :, :], ACT.Sqrt).then_inc(std_ready, 1)

            def copy_xnT(gr):
                act.wait_ge(xt_done, gr + 1)
                a.activation(xnT[:, gr * TG * P:(gr + 1) * TG * P], bank[gr % 2][:, :], ACT.Copy).then_inc(xnT_ready, 1)

            def normalise(gr):
                c = gr * TG // TC
                act.wait_ge(rstd_ready, c + 1)
                for t in range(gr * TG, gr * TG + XN_ACT):
                    last = a.activation(xn[:, t, :], x[:, t, :], ACT.Identity, bias=shift[:, t:t + 1],
                                        scale=rstd[:, c, 0, t % TC:t % TC + 1])
                last.then_inc(xn_by_act, 1)

            def copy_v(b):
                act.wait_ge(v_done, b + 1)
                a.activation(v_all[:, TB * b:TB * (b + 1), 0:E + D],
                             bank[2 + b % 2][:, 0:TB * (E + D)].rearrange("p (j d) -> p j d", j=TB), ACT.Copy).then_inc(v_copied, 1)

            sqrt_of(0)
            for c in range(NCH):
                for gr in range(c * NG // NCH, (c + 1) * NG // NCH):
                    normalise(gr)
                if c + 1 < NCH:
                    sqrt_of(c + 1)
                for gr in range(c * NG // NCH, (c + 1) * NG // NCH):
                    copy_xnT(gr)
                    for b in range((gr - LAG) * TG // TB, (gr - LAG + 1) * TG // TB):
                        if b >= 0:
                            copy_v(b)
            for b in range((NG - LAG) * TG // TB, NB):
                copy_v(b)
            act.wait_ge(max_ready, 1)
            a.activation(alpha_e[:, :], aff_max[:, :], ACT.Exp, scale=-1.0).then_inc(sig_exp, 1)

            def exp_of_k(b, par):
                act.wait_ge(k_done, b + 1)
                a.activation(k_neg[:, par, :], bank[par][:, 0:TB * P], ACT.Relu, scale=-1.0).then_inc(k_neg_ready, 1)
                wait_for(act, k_ready, b - 1)
                a.activation(k_pos[:, par, :], bank[par][:, 0:TB * P], ACT.Relu).then_inc(k_read, 1)
                act.wait_ge(k_neg_ready, b + 1)
                a.activation(k_exp[:, par, :], k_neg[:, par, :], ACT.Exp, scale=-1.0).then_inc(k_exp_ready, 1)

            def copy_kv(b, par):
                act.wait_ge(kv_done, b + 1)
                wait_for(act, kvm_ready, b - 1)
                a.activation(kv_c[:, par, :], bank[2 + par][:, 0:KVW], ACT.Copy).then_inc(kv_copied, 1)

            def part_values():
                act.wait_ge(slot_hot_ready, 1)
                a.activation(slot_val[:, :, 0, :], slot_hot[:, :, :], ACT.Identity, scale=part_no1[:, :]).then_inc(part_val_ready, 1)

            for i in range(NB + KV_LAG + 1):
                if i == PART_AT:
                    part_values()
                if i < NB:
                    exp_of_k(i, i % 2)
                if i > KV_LAG:
                    copy_kv(i - KV_LAG - 1, (i - KV_LAG - 1) % 2)

            def exp_of_q(b, par, last=False):
                act.wait_ge(q_done, b + 1)
                a.activation(q_neg[:, par, :], bank_of(Q, par, last)[:, 0:TB * P], ACT.Relu, scale=-1.0).then_inc(q_neg_ready, 1)
                act.wait_ge(q_neg_ready, b + 1)
                a.activation(q_exp[:, par, :], q_neg[:, par, :], ACT.Exp, scale=-1.0).then_inc(q_exp_ready, 1)

            def copy_headsT(b, par, last=False):
                act.wait_ge(ht_done, b + 1)
                a.activation(headsT[:, par, :], bank_of(HT, par, last)[:, 0:TB * P], ACT.Copy).then_inc(ht_copied, 1)

            def hidden(s, par, e):
                act.wait_ge(h_done, s + 1)
                for c in range(FC):
                    last = a.activation(hT[:, par, c * P:(c + 1) * P], bank[2 + par][:, c * P:(c + 1) * P], ACT.Relu,
                                        bias=b1[:, c, bass.ds(e, 1)])
                last.then_inc(h_ready, 1)

            act.wait_ge(bias_in, 16 * 2)
            act.wait_ge(expert_ready, 2)
            for s in (0, 1):
                hidden(s, s, act.value_load(ex_i[0:1, s:s + 1], min_val=0, max_val=E - 1))
            with act.Fori(0, TURNS) as k:
                for n in range(RING):
                    s, b, stage = k * RING + (n + 2), k * (RING // TPB) + n // TPB, n % TPB
                    if n % 2 == 0:
                        v = act.value_load(ex_pair[0:1, bass.ds(k * (RING // 2) + n // 2, 1)], min_val=0, max_val=E ** WORD - 1)
                    if stage == 0:
                        exp_of_q(b, n // TPB % 2)
                    if stage == 2:
                        copy_headsT(b, n // TPB % 2)
                    hidden(s, n % 2, slot(v, 2 + n % 2))
            hidden(NSLOT - 1, 0, act.value_load(ex_i[0:1, NSLOT - 1:NSLOT], min_val=0, max_val=E - 1))
            for i in range(NB - NB1 + 2):
                if i < NB - NB1:
                    exp_of_q(NB1 + i, i % 2, last=True)
                if i >= 2:
                    copy_headsT(NB1 + i - 2, i % 2, last=True)

        @block.tensor
        def _(pe):
            t_ = nc.tensor
            pe.wait_ge(ident_ready, 1)

            def transpose_x(gr):
                pe.wait_ge(xn_by_dve, gr + 1)
                pe.wait_ge(xn_by_act, gr + 1)
                wait_for(pe, xnT_ready, gr - 1)
                for j in range(TG):
                    last = t_.transpose(bank[gr % 2][:, j * P:(j + 1) * P], xn[:, gr * TG + j, :], ident[:, :])
                last.then_inc(xt_done, 1)

            def values(b):
                pe.wait_ge(xnT_ready, TB * b // TG + 1)
                wait_for(pe, v_copied, b - 1)
                for j in range(TB):
                    t = TB * b + j
                    last = t_.matmul(bank[2 + b % 2][:, j * (E + D):(j + 1) * (E + D)], xnT[:, t * P:(t + 1) * P], cent_wv[:, :],
                                     start=True, stop=True)
                last.then_inc(v_done, 1)

            for gr in range(NG):
                transpose_x(gr)
                if gr == LAG:
                    pe.wait_ge(cent_wv_in, 16 * 2)
                for b in range((gr - LAG) * TG // TB, (gr - LAG + 1) * TG // TB):
                    if b >= 0:
                        values(b)
            for b in range((NG - LAG) * TG // TB, NB):
                values(b)

            def project_k(b):
                if b > 1:
                    pe.wait_ge(k_read, b - 1)
                for j in range(TB):
                    t = TB * b + j
                    last = t_.matmul(bank[b % 2][:, j * P:(j + 1) * P], xnT[:, t * P:(t + 1) * P], wk[:, :], start=True, stop=True)
                last.then_inc(k_done, 1)

            def keys_values(b):
                pe.wait_ge(k_ready, b + 1)
                wait_for(pe, kv_copied, b - 1)
                for j in range(TB):
                    last = t_.matmul(bank[2 + b % 2][:, 0:KVW], feat_k[:, TB * b + j, :], v_all[:, TB * b + j, E:E + KVW],
                                     start=(j == 0), stop=(j == TB - 1))
                last.then_inc(kv_done, 1)

            def ranks():
                pe.wait_ge(const_ready, 10)
                pe.wait_ge(chosen_ready, 1)
                hot = chosen[:, :, :].rearrange("p e t -> p (e t)")
                t_.matmul(bank[7][:, 0:E * NT], before[:, :], hot, start=True, stop=True)
                t_.matmul(bank[7][:, E * NT:2 * E * NT], ones[:, :], hot, start=True, stop=True).then_inc(ranks_done, 1)

            def tokens():
                pe.wait_ge(part_val_ready, 1)
                pe.wait_ge(tile_val_ready, 1)
                for t in range(NT):
                    if t % LANES_PIECE == 0:
                        pe.wait_ge(lane_ready, t // LANES_PIECE + 1)
                    last = t_.matmul(bank[7][:, 0:2 * NSLOT], lane_hot[:, t, :],
                                     slot_val[:, t, :, :].rearrange("p a s -> p (a s)"), start=(t == 0), stop=(t == NT - 1))
                last.then_inc(tok_done, 1)

            pe.wait_ge(attw_in, 16 * 3)
            pe.wait_ge(aug_ready, 1)
            pe.wait_ge(xnT_ready, NG)
            pe.wait_ge(v_copied, NB)
            for i in range(NB + KV_LAG):
                if i == RANKS_AT:
                    ranks()
                if i == TOKENS_AT:
                    tokens()
                if i < NB:
                    project_k(i)
                if i >= KV_LAG:
                    keys_values(i - KV_LAG)

            def project_q(b, par, last=False):
                t_.matmul(bank_of(Q, par, last)[:, 0:TB * P], wq[:, :], some(xnT, b * (TB * P), TB * P), start=True, stop=True)\
                  .then_inc(q_done, 1)

            def num(b, par, last=False):
                pe.wait_ge(q_ready, b + 1)
                if not last or b == NB1:
                    pe.wait_ge(base_ready, b + 1)
                for j in range(TB):
                    mm = t_.matmul(bank_of(NUM, par, last)[:, j * KVW:(j + 1) * KVW], feat_q[:, par, j * P:(j + 1) * P],
                                   some(kv_m, b, 1).rearrange("p b c -> p (b c)"), start=True, stop=True)
                mm.then_inc(num_done, 1)

            def turn_heads(b, par, last=False):
                pe.wait_ge(heads_ready, b + 1)
                if last:
                    pe.wait_ge(ht_copied, b)
                for j in range(TB):
                    mm = t_.transpose(bank_of(HT, par, last)[:, j * P:(j + 1) * P], heads[:, j, :], ident[:, :])
                mm.then_inc(ht_done, 1)

            def out_project(b, par, last=False):
                pe.wait_ge(ht_copied, b + 1)
                if last:
                    pe.wait_ge(base_ready, b + 1)
                for j in range(TB):
                    mm = t_.matmul(bank_of(OUT, par, last)[:, j * D:(j + 1) * D], headsT[:, par, j * P:(j + 1) * P], wo[:, :],
                                   start=True, stop=True)
                mm.then_inc(att_done, 1)

            def turn_rows(s, par, place):
                pe.wait_ge(gathered, s + 1)
                t_.transpose(bank[par][:, 0:P], rows[:, place, :], ident[:, :]).then_inc(zt_done, 1)

            def hidden(s, par):
                pe.wait_ge(zt_ready, s + 1)
                pe.wait_ge(w1_ready, s + 1)
                for c in range(FC):
                    last = t_.matmul(bank[2 + par][:, c * P:(c + 1) * P], w1_now[:, par, c * P:(c + 1) * P], zT[:, par, :],
                                     start=True, stop=True)
                last.then_inc(h_done, 1)

            def second(s, par, e):
                pe.wait_ge(h_ready, s + 1)
                wait_for(pe, y_ready, s - 1)
                for c in range(FC):
                    last = t_.matmul(bank[6 + par][:, 0:D], hT[:, par, c * P:(c + 1) * P],
                                     w2[:, bass.ds(e * (FC * D) + c * D, D)], start=(c == 0), stop=(c == FC - 1))
                last.then_inc(y_done, 1)

            pe.wait_ge(k_read, NB)
            pe.wait_ge(kvm_ready, NB)
            pe.wait_ge(index_ready, 1)
            pe.wait_ge(w2_in, 16)
            pe.wait_ge(expert_ready, 2)

            def expert_of(s):
                return pe.value_load(ex_i[0:1, s:s + 1], min_val=0, max_val=E - 1)

            turn_rows(0, 0, 0)
            turn_rows(1, 1, 1)
            hidden(0, 0)
            turn_rows(2, 0, 2)
            hidden(1, 1)
            second(0, 0, expert_of(0))
            with pe.Fori(0, TURNS) as k:
                for n in range(RING):
                    s, par, place = k * RING + (n + 2), n % 2, (n + 2) % RING
                    b, stage, b_par = k * (RING // TPB) + n // TPB, n % TPB, n // TPB % 2
                    if par == 0:
                        v = pe.value_load(ex_pair[0:1, bass.ds(k * (RING // 2) + n // 2, 1)], min_val=0, max_val=E ** WORD - 1)
                    (project_q, num, turn_heads)[stage](b, b_par)
                    turn_rows(s + 1, 1 - par, (place + 1) % RING)
                    hidden(s, par)
                    if stage == 2:
                        out_project(b, b_par)
                    second(s - 1, 1 - par, slot(v, 1 + par))
            hidden(NSLOT - 1, 0)
            second(NSLOT - 2, 1, expert_of(NSLOT - 2))
            second(NSLOT - 1, 0, expert_of(NSLOT - 1))

            for i in range(NB - NB1 + 3):
                b, par = NB1 + i, i % 2
                if i < NB - NB1:
                    project_q(b, par, last=True)
                if 1 <= i < NB - NB1 + 1:
                    num(b - 1, 1 - par, last=True)
                if 2 <= i < NB - NB1 + 2:
                    turn_heads(b - 2, par, last=True)
                if i >= 3:
                    out_project(b - 3, 1 - par, last=True)

        @block.vector
        def _(dve):
            v_ = nc.vector

            def statistics(c):
                if c < NCH:
                    dve.wait_ge(x_in[c], 16)
                    for j in range(TC):
                        ins = v_.bn_stats(stats[:, c % 2, j, :], x[:, c * TC + j, :])
                        if j == TC - 1:
                            ins.then_inc(stat_done, 1)
                        yield

            chained = [0]

            def step(ins, filling):
                chained[0] += 1
                ins.then_inc(chain, 1)
                next(filling, None)
                dve.wait_ge(chain, chained[0])

            def moments(c, filling):
                st = stats[:, c % 2, :, :]
                mean_c = mean[:, c * TC:(c + 1) * TC]
                var = ms_b[:, 1, :]
                dve.wait_ge(stat_done, c + 1)
                v_.tensor_tensor(ms_a[:, 0, :], st[:, :, 1], st[:, :, 4], ALU.add)
                v_.tensor_tensor(ms_a[:, 1, :], st[:, :, 1], st[:, :, 4], ALU.subtract)
                step(v_.tensor_tensor(ms_a[:, 2, :], st[:, :, 2], st[:, :, 5], ALU.add), filling)
                v_.tensor_scalar(mean_c, ms_a[:, 0, :], 0.5, None, ALU.mult)
                step(v_.scalar_tensor_tensor(ms_b[:, 0, :], ms_a[:, 1, :], 0.25, ms_a[:, 1, :], ALU.mult, ALU.mult), filling)
                step(v_.scalar_tensor_tensor(var, ms_a[:, 2, :], 1.0 / D, ms_b[:, 0, :], ALU.mult, ALU.add), filling)
                v_.tensor_scalar(var_e[:, c, 0, :], var, 1.0, EPS_LN, ALU.mult, ALU.add)
                v_.tensor_scalar(var_e[:, c, 1, :], var, 1.0 + EPS_LN, EPS_LN * EPS_LN, ALU.mult, ALU.add).then_inc(var_ready, 1)

            def rsqrts(c, filling):
                part = slice(c * TC, (c + 1) * TC)
                dve.wait_ge(std_ready, c + 1)
                dve.wait_ge(var_ready, c + 1)
                step(v_.reciprocal(rinv[:, :, :], std[:, c, :, :]), filling)
                step(v_.tensor_tensor(nw_a[:, :, :], rinv[:, :, :], rinv[:, :, :], ALU.mult), filling)
                step(v_.tensor_tensor(nw_b[:, :, :], nw_a[:, :, :], var_e[:, c, :, :], ALU.mult), filling)
                step(v_.tensor_scalar(nw_a[:, :, :], nw_b[:, :, :], -0.5, 1.5, ALU.mult, ALU.add), filling)
                step(v_.tensor_tensor(rstd[:, c, :, :], rinv[:, :, :], nw_a[:, :, :], ALU.mult), filling)
                v_.scalar_tensor_tensor(shift[:, part], mean[:, part], -1.0, rstd[:, c, 0, :], ALU.mult, ALU.mult)\
                  .then_inc(rstd_ready, 1)
                step(v_.tensor_tensor(nw_c[:, :], var_e[:, c, 0, :], rstd[:, c, 0, :], ALU.mult), filling)
                v_.tensor_tensor(zscale[:, part], nw_c[:, :], rstd[:, c, 1, :], ALU.mult).then_inc(zscale_ready, 1)

            def normalise(c):
                for j in range(TC):
                    if j % TG >= XN_ACT:
                        t = c * TC + j
                        ins = v_.tensor_scalar(xn[:, t, :], x[:, t, :], mean[:, t:t + 1], rstd[:, c, 0, j:j + 1], ALU.subtract, ALU.mult)
                        if j % TG == TG - 1:
                            ins.then_inc(xn_by_dve, 1)
                        yield

            def finish(work):
                for _ in work:
                    pass

            finish(statistics(0))
            filling = statistics(1)
            moments(0, filling)
            for c in range(NCH):
                rsqrts(c, filling)
                finish(filling)
                filling = normalise(c)
                if c + 1 < NCH:
                    moments(c + 1, filling)
                finish(filling)
                filling = statistics(c + 2)

            steps = [0]

            def then(ins):
                steps[0] += 1
                ins.then_inc(route, 1)
                dve.wait_ge(route, steps[0])

            def per_e(v):
                return v.unsqueeze(2).to_broadcast([P, E, NT])

            def per_t(v):
                return v.unsqueeze(1).to_broadcast([P, E, NT])

            def t_e(v):
                return v.rearrange("p e t -> p t e")

            rank_p = bank[7][:, 0:E * NT].rearrange("p (e t) -> p e t", e=E)

            aff = v_all[:, :, 0:E]

            def choose():
                dve.wait_ge(v_copied, NB)
                v_.tensor_reduce(aff_max[:, :], aff, AX.X, ALU.max).then_inc(max_ready, 1)
                dve.wait_ge(max_ready, 1)
                dve.wait_ge(const_ready, 10)
                then(v_.tensor_tensor(rt_a[:, :, :], aff.rearrange("p t e -> p e t"), per_t(aff_max[:, :]), ALU.is_equal))
                then(v_.tensor_tensor(rt_b[:, :, :], rt_a[:, :, :], rank_e[:, :, :], ALU.mult))
                then(v_.tensor_reduce(first[:, :], t_e(rt_b[:, :, :]), AX.X, ALU.max))
                v_.tensor_tensor(chosen[:, :, :], rank_e[:, :, :], per_t(first[:, :]), ALU.is_equal).then_inc(chosen_ready, 1)

            def count():
                dve.wait_ge(ranks_done, 1)
                total_p = bank[7][:, E * NT:2 * E * NT].rearrange("p (e t) -> p e t", e=E)
                then(v_.tensor_copy(total[:, :, :], total_p))
                flat = [v[:, :, :].rearrange("p e t -> p (e t)") for v in (total, upto)]
                then(v_.tensor_tensor_scan(flat[1], ones_f[:, :], flat[0], 0.0, ALU.mult, ALU.add))
                then(v_.tensor_tensor(rt_a[:, :, :], upto[:, :, :], total[:, :, :], ALU.subtract))
                then(v_.tensor_tensor(n_e[:, :], upto[:, :, NT - 1], rt_a[:, :, 0], ALU.subtract))
                then(v_.tensor_tensor(rt_b[:, :, :], per_e(n_e[:, :]), tile_starts[:, :, :], ALU.is_gt))
                then(v_.tensor_reduce(cnt[:, :], rt_b[:, :, :], AX.X, ALU.add))
                then(v_.tensor_tensor_scan(last_t[:, :], ones_f[:, 0:E], cnt[:, :], 0.0, ALU.mult, ALU.add))
                then(v_.tensor_tensor(start_t[:, :], last_t[:, :], cnt[:, :], ALU.subtract))
                then(v_.scalar_tensor_tensor(off[:, :], start_t[:, :], float(P), rt_a[:, :, 0], ALU.mult, ALU.subtract))

            def place():
                then(v_.tensor_tensor(rt_b[:, :, :], rt_a[:, :, :], rank_p, ALU.add))
                then(v_.tensor_tensor(rt_c[:, :, :], rt_b[:, :, :], per_e(off[:, :]), ALU.add))
                then(v_.tensor_tensor(rt_a[:, :, :], rt_c[:, :, :], chosen[:, :, :], ALU.mult))
                then(v_.tensor_reduce(pos[:, :], t_e(rt_a[:, :, :]), AX.X, ALU.add))
                then(v_.tensor_copy(pos_i[:, :], pos[:, :]))
                v_.tensor_scalar(hi_i[:, :], pos_i[:, :], 7, None, ALU.arith_shift_right)
                then(v_.tensor_scalar(lo_i[:, :], pos_i[:, :], P - 1, None, ALU.bitwise_and))
                v_.tensor_copy(lo_f[:, :], lo_i[:, :])
                then(v_.tensor_copy(hi_f[:, :], hi_i[:, :]))

            def hot_lanes():
                for t in range(NT):
                    ins = v_.tensor_scalar(lane_hot[:, t, :], lane[:, :], lo_f[:, t:t + 1], None, ALU.is_equal)
                    if t % LANES_PIECE == LANES_PIECE - 1:
                        ins.then_inc(lane_ready, 1)

            def hot_slots():
                v_.tensor_tensor(slot_hot[:, :, :], slot_no[:, 0:NSLOT].unsqueeze(1).to_broadcast([P, NT, NSLOT]),
                                 hi_f[:, :].unsqueeze(2).to_broadcast([P, NT, NSLOT]), ALU.is_equal).then_inc(slot_hot_ready, 1)

            def weights():
                dve.wait_ge(sig_exp, 1)
                then(v_.tensor_scalar(alpha_1[:, :], alpha_e[:, :], 1.0, None, ALU.add))
                v_.reciprocal(alpha[:, :], alpha_1[:, :]).then_inc(alpha_ready, 1)

            def slot_experts():
                then(v_.tensor_tensor(ex_cmp[:, :, :], slot_no[0:1, :].unsqueeze(2).to_broadcast([1, NSLOT + 1, E]),
                                      last_t[0:1, :].unsqueeze(1).to_broadcast([1, NSLOT + 1, E]), ALU.is_ge))
                then(v_.tensor_reduce(ex_f[:, :], ex_cmp[:, :, :], AX.X, ALU.add))
                then(v_.tensor_scalar(ex_m[:, :], ex_f[:, :], float(E - 1), None, ALU.min))
                v_.tensor_copy(ex_i[:, :], ex_m[:, :]).then_inc(expert_ready, 1)
                ev = [ex_m[:, j:j + 2 * PAIRS - 1:2] for j in range(WORD)]
                word = ev[WORD - 1]
                for j in reversed(range(1, WORD - 1)):
                    then(v_.scalar_tensor_tensor(ex_p[j % 2][:, :], word, float(E), ev[j], ALU.mult, ALU.add))
                    word = ex_p[j % 2][:, :]
                v_.scalar_tensor_tensor(ex_pair[:, :], word, float(E), ev[0], ALU.mult, ALU.add).then_inc(expert_ready, 1)

            def slot_tokens():
                dve.wait_ge(tok_done, 1)
                then(v_.tensor_copy(tok_c[:, :, :], bank[7][:, 0:2 * NSLOT].rearrange("p (a s) -> p a s", a=2)))
                then(v_.scalar_tensor_tensor(tok_f[:, :], tok_c[:, 1, :], float(P), tok_c[:, 0, :], ALU.mult, ALU.add))
                v_.tensor_scalar(gather_at[:, :], tok_f[:, :], -1.0, 0.0, ALU.add, ALU.max)
                then(v_.tensor_scalar(tok_neg[:, :], tok_f[:, :], 0.5, float(2 * NTOK), ALU.is_lt, ALU.mult))
                v_.scalar_tensor_tensor(scatter_at[:, :], tok_f[:, :], -1.0, tok_neg[:, :], ALU.add, ALU.add).then_inc(index_ready, 1)

            def features_q(b, par, last=False):
                dve.wait_ge(q_exp_ready, b + 1)
                v_.scalar_tensor_tensor(feat_q[:, par, :], bank_of(Q, par, last)[:, 0:TB * P], 0.0, q_exp[:, par, :], ALU.max, ALU.add)\
                  .then_inc(q_ready, 1)

            def divide(b, par, last=False):
                dve.wait_ge(num_done, b + 1)
                nd = bank_of(NUM, par, last)[:, 0:TB * KVW].rearrange("p (j c) -> p j c", j=TB)
                v_.tensor_scalar(den[:, :, :], nd[:, :, D:KVW], EPS_ATT, None, ALU.add).then_inc(den_ready, 1)
                dve.wait_ge(den_ready, b + 1)
                v_.reciprocal(rden[:, :, :], den[:, :, :]).then_inc(rden_ready, 1)
                dve.wait_ge(rden_ready, b + 1)
                if last:
                    dve.wait_ge(ht_done, b)
                for j in range(TB):
                    ins = v_.tensor_tensor(heads[:, j, :].rearrange("p (h m) -> p h m", h=H),
                                            nd[:, j, 0:D].rearrange("p (h m) -> p h m", h=H),
                                            rden[:, j, :].unsqueeze(2).to_broadcast([P, H, HD]), ALU.mult)
                ins.then_inc(heads_ready, 1)

            def add_attention(b, par, last=False):
                dve.wait_ge(att_done, b + 1)
                two = some(base, b * TB, TB)
                v_.tensor_tensor(two, bank_of(OUT, par, last)[:, 0:TB * D].rearrange("p (j d) -> p j d", j=TB), two, ALU.add).then_inc(base_ready, 1)

            def turned(s, par, e):
                dve.wait_ge(zt_done, s + 1)
                wait_for(dve, h_done, s - 1)
                v_.tensor_scalar(zT[:, par, :], bank[par][:, 0:P], ln_g[:, bass.ds(e, 1)], ln_b[:, bass.ds(e, 1)],
                                 ALU.mult, ALU.add).then_inc(zt_ready, 1)
                v_.tensor_copy(w1_now[:, par, :], w1[:, bass.ds(e * F, F)]).then_inc(w1_ready, 1)

            def result(s, par, e):
                dve.wait_ge(y_done, s + 1)
                v_.tensor_tensor(some(y_rows, s, 1).rearrange("p s d -> p (s d)"), bank[6 + par][:, 0:D], b2[:, bass.ds(e * D, D)], ALU.add).then_inc(y_ready, 1)

            for piece in (choose, count, place, hot_slots, hot_lanes, slot_tokens, slot_experts, weights):
                piece()

            def expert_of(s):
                return dve.value_load(ex_i[0:1, s:s + 1], min_val=0, max_val=E - 1)

            dve.wait_ge(expert_ready, 2)
            dve.wait_ge(small_in, 16 * 2)
            dve.wait_ge(bias_in, 16 * 2)
            dve.wait_ge(w1_in, 16)
            e0, e1 = expert_of(0), expert_of(1)
            turned(0, 0, e0)
            turned(1, 1, e1)
            turned(2, 0, expert_of(2))
            with dve.Fori(0, TURNS) as k:
                for n in range(RING):
                    s, b, stage = k * RING + (n + 2), k * (RING // TPB) + n // TPB, n % TPB
                    if n % 2 == 0:
                        v = dve.value_load(ex_pair[0:1, bass.ds(k * (RING // 2) + n // 2, 1)], min_val=0, max_val=E ** WORD - 1)
                    result(s - 2, n % 2, slot(v, n % 2))
                    turned(s + 1, 1 - n % 2, slot(v, n % 2 + 3))
                    if stage == 0:
                        features_q(b, n // TPB % 2)
                    else:
                        (divide, add_attention)[stage - 1](b, n // TPB % 2)
            for s in range(NSLOT - 3, NSLOT):
                result(s, s % 2, expert_of(s))

            def add_experts(b):
                dve.wait_ge(y_in[b * TB // TC], 16)
                dve.wait_ge(base_ready, b + 2)
                for t in range(TB * b, TB * (b + 1)):
                    last = v_.scalar_tensor_tensor(base[:, t, :], y_back[:, t, :], alpha[:, t:t + 1], base[:, t, :], ALU.mult, ALU.add)
                last.then_inc(dve_added, 1)

            for i in range(NB - NB1 + 3):
                b, par = NB1 + i, i % 2
                if i < NB - NB1:
                    features_q(b, par, last=True)
                if 1 <= i < NB - NB1 + 1:
                    divide(b - 1, 1 - par, last=True)
                if i >= 3:
                    add_attention(b - 3, 1 - par, last=True)
                for b in DVE_ADDS.get(i, ()):
                    add_experts(b)


def kernel(L0_attn_x, L0_attn_Wq, L0_attn_Wk, L0_attn_Wv, L0_attn_Wo, L0_ffn_centroids, L0_ffn_ln_g, L0_ffn_ln_b,
           L0_ffn_w1, L0_ffn_b1, L0_ffn_w2, L0_ffn_b2):
    import numpy as np
    import concourse.bacc as bacc
    from concourse.bass_utils import run_bass_kernel_spmd

    P = 128
    x = np.ascontiguousarray(L0_attn_x)
    w1, b1, w2 = (np.asarray(v) for v in (L0_ffn_w1, L0_ffn_b1, L0_ffn_w2))
    E, F, D = w1.shape
    C = F // P
    laid = {
        "x": x,
        "wqT": np.asarray(L0_attn_Wq).T, "wkT": np.asarray(L0_attn_Wk).T,
        "wvT": np.asarray(L0_attn_Wv).T, "woT": np.asarray(L0_attn_Wo).T,
        "centT": np.asarray(L0_ffn_centroids).T, "gT": np.asarray(L0_ffn_ln_g).T, "bT": np.asarray(L0_ffn_ln_b).T,
        "w1T": w1.transpose(2, 0, 1).reshape(D, E * F),
        "b1T": b1.reshape(E, C, P).transpose(2, 1, 0),
        "w2T": w2.reshape(E, D, C, P).transpose(3, 0, 2, 1).reshape(P, E * C * D),
        "b2": np.asarray(L0_ffn_b2),
    }
    nc = bacc.Bacc("TRN2", target_bir_lowering=False, num_devices=1)
    arrays, args = {}, []
    for name, a in laid.items():
        a = np.ascontiguousarray(a)
        arrays["in_" + name] = a
        args.append(nc.dram_tensor("in_" + name, a.shape, mybir.dt.from_np(a.dtype), kind="ExternalInput").ap())
    args.append(nc.dram_tensor("out", x.shape, mybir.dt.from_np(x.dtype), kind="ExternalOutput").ap())
    linear_attention_and_routed_experts(nc, *args)
    r = run_bass_kernel_spmd(nc, [arrays], core_ids=[0])
    return r.results[0]["out"]
```

```python
import concourse.bass as bass
from concourse import mybir
from contextlib import ExitStack


def linear_attention_and_routed_experts(
    nc, x_dram, wq_dram, wk_dram, wv_dram, wo_dram, cent_dram, g_dram, b_dram, w1_dram, b1_dram, w2_dram, b2_dram, out_dram,
):
    f32, bf16, i32 = mybir.dt.float32, mybir.dt.bfloat16, mybir.dt.int32
    ALU = mybir.AluOpType
    ACT = mybir.ActivationFunctionType
    AX = mybir.AxisListType

    P = 128
    NB, NS, D = x_dram.shape
    NTOK = NB * NS
    NT = NTOK // P
    TB = NS // P
    _, FC, E = b1_dram.shape
    F = FC * P
    H = 16
    HD = D // H
    KVW = D + H
    NSLOT = NT + E - 1
    TPB = 4
    EPS_LN, EPS_ATT = 1e-5, 1e-6
    NCH = 4
    TC = NT // NCH
    X_FIRST = 4
    TG = 4
    XN_ACT = (1, 2, 2, 1)
    V_BANKS = 3
    LAG = 1
    NG = NT // TG
    AHEAD = 4
    RING = 12
    PAIRS = (NSLOT - 3) // 2
    TURNS = 2 * PAIRS // RING
    EARLY = 1
    NB1 = EARLY + 2 * PAIRS // TPB
    KV_BANKS = 3
    KV_LAG = 3
    RANKS_AT, TOKENS_AT, PART_AT, TILE_AT = 2, 10, 8, 8
    K_POOL = 12
    WORD = 5
    LANES_PIECE = 8
    POOL_ADDS = 8
    DVE_ADDS = {4: (8,), 5: (9,), 6: (10, 11), 7: (12, 13), 8: (14, 15)}
    ACT_SCALES = {4: (0,), 5: (1, 2), 6: (3, 4, 5), 7: (6, 7)}
    DVE_ORDER = sum(DVE_ADDS.values(), ())
    YB = 2
    Y_ORDER = (0, 1, 4, 2, 5, 3, 6, 7)
    STORES = ((0, 1), (8, 1), (1, 2), (9, 1), (3, 1), (10, 2), (4, 2), (12, 2), (6, 2), (14, 2))
    assert D == P and TB == 2 and NSLOT == 2 * PAIRS + 3 and 2 * PAIRS == TURNS * RING and RING % TPB == 0

    x_t = x_dram.rearrange("b (j p) d -> p (b j) d", p=P)
    out_t = out_dram.rearrange("b (j p) d -> p (b j) d", p=P)
    z_dram = nc.dram_tensor("z_rows", (NTOK, D), f32, kind="Internal").ap()
    y_dram = nc.dram_tensor("y_rows", (NTOK, D), f32, kind="Internal").ap()
    z_t = z_dram.rearrange("(t p) d -> p t d", p=P)
    y_t = y_dram.rearrange("(t p) d -> p t d", p=P)

    ctx = ExitStack()
    with ctx:
        def sb(name, shape, dt=f32):
            return ctx.enter_context(nc.sbuf_tensor(name, shape, dt))

        def sem(name):
            return ctx.enter_context(nc.semaphore(name))

        bank = [ctx.enter_context(nc.psum_tensor(f"bank{i}", [P, 512], f32)) for i in range(8)]

        wq, wk, wo = sb("wq", [P, D]), sb("wk", [P, D]), sb("wo", [P, D])
        cent_wv = sb("cent_wv", [P, E + D])
        ln_g, ln_b = sb("ln_g", [P, E]), sb("ln_b", [P, E])
        w1 = sb("w1", [P, E * F])
        w2 = sb("w2", [P, E * FC * D])
        b1 = sb("b1", [P, FC, E])
        b2 = sb("b2", [P, E * D])
        ident = sb("ident", [P, P])
        head_mask = sb("head_mask", [P, KVW])
        before = sb("before", [P, P], bf16)
        ones = sb("ones", [P, P], bf16)
        lane = sb("lane", [P, P], bf16)
        rank_e = sb("rank_e", [P, E, NT])
        slot_no = sb("slot_no", [P, NSLOT + 1])
        tile_no = sb("tile_no", [P, NT])
        part_no1 = sb("part_no1", [P, 1])
        ones_f = sb("ones_f", [P, E * NT])
        x = sb("x", [P, NT, D])
        xn_y = sb("xn_and_y_tiles", [P, NSLOT, D])
        xn = xn_y[:, 0:NT, :]
        z = sb("z", [P, NT, D])
        base = sb("base", [P, NT, D])
        xnT = sb("xnT", [P, NT * P])
        stats = sb("stats", [P, 2, TC, 6])
        ms_a, ms_b = sb("ms_a", [P, 3, TC]), sb("ms_b", [P, 2, TC])
        mean = sb("mean", [P, NT])
        shift = sb("shift", [P, NT])
        zscale = sb("zscale", [P, NT])
        nw_c = sb("nw_c", [P, TC])
        var_e = sb("var_e", [P, NCH, 2, TC])
        std = sb("std", [P, NCH, 2, TC])
        nw_a, nw_b = sb("nw_a", [P, 2, TC]), sb("nw_b", [P, 2, TC])
        rstd = sb("rstd", [P, NCH, 2, TC])
        rinv = sb("rinv", [P, 2, TC])
        aff_max = sb("aff_max", [P, NT])
        alpha_e = sb("alpha_e", [P, NT])
        alpha_1 = sb("alpha_1", [P, NT])
        alpha = sb("alpha", [P, NT])
        rt_a, rt_b, rt_c = sb("rt_a", [P, E, NT]), sb("rt_b", [P, E, NT]), sb("rt_c", [P, E, NT])
        first = sb("first", [P, NT])
        chosen = sb("chosen", [P, E, NT], bf16)
        upto = sb("upto", [P, E * NT + 1])
        n_i, cnt_i = sb("n_i", [P, E], i32), sb("cnt_i", [P, E], i32)
        cnt, last_t, start_t, off = (sb(n, [P, E]) for n in ("cnt", "last_t", "start_t", "off"))
        pos = sb("pos", [P, NT])
        pos_i, hi_i, lo_i = sb("pos_i", [P, NT], i32), sb("hi_i", [P, NT], i32), sb("lo_i", [P, NT], i32)
        hi_f, lo_f = sb("hi_f", [P, NT]), sb("lo_f", [P, NT])
        lane_hot = sb("lane_hot", [P, NT, P], bf16)
        slot_hot = sb("slot_hot", [P, NT, NSLOT], bf16)
        slot_val = sb("slot_val", [P, NT, 2, NSLOT], bf16)
        tok_c = sb("tok_c", [P, 2, NSLOT])
        tok_f, tok_neg = sb("tok_f", [P, NSLOT]), sb("tok_neg", [P, NSLOT])
        gather_at, scatter_at = sb("gather_at", [P, NSLOT], i32), sb("scatter_at", [P, NSLOT], i32)
        ex_cmp = sb("ex_cmp", [1, NSLOT + 1, E])
        ex_f, ex_m = sb("ex_f", [1, NSLOT + 1]), sb("ex_m", [1, NSLOT + 1])
        ex_p = [sb(f"ex_p{i}", [1, PAIRS]) for i in range(2)]
        ex_i, ex_pair = sb("ex_i", [1, NSLOT + 1], i32), sb("ex_pair", [1, PAIRS], i32)
        v_all = sb("v_all", [P, NT, E + KVW])
        feat_k = x
        kv_all = sb("kv_all", [P, NB, KVW])
        k_neg, k_pos, k_exp = (sb(n, [P, 2, TB * P]) for n in ("k_neg", "k_pos", "k_exp"))
        kv_m = sb("kv_m", [P, 2, KVW])
        q_neg, q_exp, feat_q = k_neg, k_exp, k_pos
        den, rden = sb("den", [P, TB, H]), sb("rden", [P, TB, H])
        heads = sb("heads", [P, TB, D])
        headsT = sb("headsT", [P, 2, TB * P])
        rows = sb("rows", [P, RING, D])
        y_rows = xn_y
        zT = sb("zT", [P, 2, P])
        w1_now = sb("w1_now", [P, 2, F])
        hT = sb("hT", [P, 2, F])
        y_back = z

        x_first_in = sem("x_first_in")
        x_in = [sem(f"x_in{c}") for c in range(NCH)]
        cent_wv_in, small_in, bias_in, attw_in, w1_in, w2_in = sem("cent_wv_in"), sem("small_in"), sem("bias_in"), sem("attw_in"), sem("w1_in"), sem("w2_in")
        z_out = sem("z_out")
        gather_in = [sem(f"gather_in{i}") for i in range(AHEAD)]
        y_out = sem("y_out")
        y_in = [sem(f"y_in{c}") for c in range(NB // YB)]
        out_done = sem("out_done")
        const_step, const_ready, ident_ready = sem("const_step"), sem("const_ready"), sem("ident_ready")
        aug_ready = sem("aug_ready")
        stat_done, chain, var_ready, std_ready = sem("stat_done"), sem("chain"), sem("var_ready"), sem("std_ready")
        xn_by_dve, xn_by_act, z_ready = sem("xn_by_dve"), sem("xn_by_act"), sem("z_ready")
        rstd_ready = sem("rstd_ready")
        zscale_ready = sem("zscale_ready")
        xt_done, xnT_ready = sem("xt_done"), sem("xnT_ready")
        route, max_ready, sig_exp, chosen_ready = (sem(n) for n in ("route", "max_ready", "sig_exp", "chosen_ready"))
        alpha_ready, ranks_done, tok_done, index_ready, expert_ready = (
            sem(n) for n in ("alpha_ready", "ranks_done", "tok_done", "index_ready", "expert_ready"))
        lane_ready, slot_hot_ready, part_val_ready, tile_val_ready = (
            sem(n) for n in ("lane_ready", "slot_hot_ready", "part_val_ready", "tile_val_ready"))
        v_done, v_copied = sem("v_done"), sem("v_copied")
        k_done, k_neg_ready, k_read, k_exp_ready, k_ready, kv_done, kv_copied = (
            sem(n) for n in ("k_done", "k_neg_ready", "k_read", "k_exp_ready", "k_ready", "kv_done", "kv_copied"))
        k_by_dve, last_kv_ready = sem("k_by_dve"), sem("last_kv_ready")
        q_done, q_neg_ready, q_exp_ready, q_ready = (sem(n) for n in ("q_done", "q_neg_ready", "q_exp_ready", "q_ready"))
        num_done, den_ready, rden_ready, heads_ready = (sem(n) for n in ("num_done", "den_ready", "rden_ready", "heads_ready"))
        ht_done, ht_copied, att_done = (sem(n) for n in ("ht_done", "ht_copied", "att_done"))
        last_base_ready = sem("last_base_ready")
        base_ready = sem("base_ready")
        gathered, zt_done, zt_ready, w1_ready, h_done, h_ready, y_done, y_ready = (
            sem(n) for n in ("gathered", "zt_done", "zt_ready", "w1_ready", "h_done", "h_ready", "y_done", "y_ready"))
        scaled, pool_added, dve_added = sem("scaled"), sem("pool_added"), sem("dve_added")

        block = ctx.enter_context(nc.Block())

        Q, NUM, HT, OUT = range(4)

        def bank_of(stage, par, last):
            return bank[((par, 4 - par, 5, 2) if last else (5, 4, 5, 4))[stage]]

        def wait_for(eng, s, n):
            if not isinstance(n, int) or n > 0:
                eng.wait_ge(s, n)

        def wait_batch(eng, by_pool, by_dve, b):
            if 0 <= b < K_POOL:
                eng.wait_ge(by_pool, b + 1)
            elif b >= K_POOL:
                eng.wait_ge(by_dve, b - K_POOL + 1)

        def some(v, first, n):
            return v[:, first:first + n] if isinstance(first, int) else v[:, bass.ds(first, n)]

        def slot(v, j):
            return (v >> (3 * j)) & 7 if j else v & 7

        @block.sync
        def _(sp):
            sp.dma_start(x[:, 0:X_FIRST, :], x_t[:, 0:X_FIRST, :]).then_inc(x_first_in, 16)
            for c in range(NCH):
                first = X_FIRST if c == 0 else c * TC
                sp.dma_start(x[:, first:(c + 1) * TC, :], x_t[:, first:(c + 1) * TC, :]).then_inc(x_in[c], 16)
                if c == 0:
                    sp.dma_start(cent_wv[:, 0:E], cent_dram).then_inc(cent_wv_in, 16)
                    sp.dma_start(cent_wv[:, E:E + D], wv_dram).then_inc(cent_wv_in, 16)
            for dst, src in ((ln_g, g_dram), (ln_b, b_dram)):
                sp.dma_start(dst[:, :], src).then_inc(small_in, 16)
            for dst, src in ((wq, wq_dram), (wk, wk_dram), (wo, wo_dram)):
                sp.dma_start(dst[:, :], src).then_inc(attw_in, 16)
            sp.dma_start(b1[:, :, :], b1_dram).then_inc(bias_in, 16)
            sp.dma_start(b2[:, :], b2_dram.rearrange("e d -> (e d)").partition_broadcast(P)).then_inc(bias_in, 16)
            sp.dma_start(w1[:, :], w1_dram).then_inc(w1_in, 16)
            for c in range(NCH):
                sp.wait_ge(z_ready, c + 1)
                sp.dma_start(z_t[:, c * TC:(c + 1) * TC, :], z[:, c * TC:(c + 1) * TC, :]).then_inc(z_out, 16)
            sp.dma_start(w2[:, :], w2_dram).then_inc(w2_in, 16)
            sp.wait_ge(y_out, 16 * NSLOT)
            for c in Y_ORDER:
                sp.dma_start(y_back[:, c * YB * TB:(c + 1) * YB * TB, :], y_t[:, c * YB * TB:(c + 1) * YB * TB, :]).then_inc(y_in[c], 16)
            for b, n in STORES:
                if b < POOL_ADDS:
                    sp.wait_ge(pool_added, b + n)
                else:
                    sp.wait_ge(dve_added, DVE_ORDER.index(b + n - 1) + 1)
                sp.dma_start(out_t[:, TB * b:TB * (b + n), :], base[:, TB * b:TB * (b + n), :]).then_inc(out_done, 16)
            sp.wait_ge(out_done, 16 * len(STORES))

        @block.gpsimd
        def _(pool):
            g = nc.gpsimd
            g.memset(ident[:, :], 0.0).then_inc(const_step, 1)
            g.memset(head_mask[:, :], 1.0).then_inc(const_step, 1)
            g.memset(before[:, :], 1.0).then_inc(const_step, 1)
            pool.wait_ge(const_step, 3)
            g.affine_select(out=ident[:, :], in_=ident[:, :], compare_op=ALU.not_equal, fill=1.0, base=0,
                            pattern=[[-1, P]], channel_multiplier=1).then_inc(ident_ready, 1)
            for col, shape in ((head_mask[:, 0:D], [0, HD]), (head_mask[:, D:KVW], [0, 1])):
                pat = [[-HD, H], shape]
                v = col.rearrange("p (h j) -> p h j", h=H)
                g.affine_select(out=v, in_=v, compare_op=ALU.is_ge, fill=0.0, base=0,
                                pattern=pat, channel_multiplier=1).then_inc(const_step, 1)
            pool.wait_ge(const_step, 5)
            for col, shape in ((head_mask[:, 0:D], [0, HD]), (head_mask[:, D:KVW], [0, 1])):
                v = col.rearrange("p (h j) -> p h j", h=H)
                g.affine_select(out=v, in_=v, compare_op=ALU.is_ge, fill=0.0, base=HD - 1,
                                pattern=[[HD, H], shape], channel_multiplier=-1).then_inc(const_ready, 1)
            g.affine_select(out=before[:, :], in_=before[:, :], compare_op=ALU.is_ge, fill=0.0, base=-1,
                            pattern=[[1, P]], channel_multiplier=-1).then_inc(const_ready, 1)
            fine = {"allow_small_or_imprecise_dtypes": True}
            g.iota(lane[:, :], pattern=[[1, P]], base=0, channel_multiplier=0, **fine).then_inc(const_ready, 1)
            g.iota(rank_e[:, :, :], pattern=[[-1, E], [0, NT]], base=E, channel_multiplier=0, **fine).then_inc(const_ready, 1)
            g.memset(upto[:, 0:1], 0.0).then_inc(const_ready, 1)
            g.iota(slot_no[:, :], pattern=[[1, NSLOT + 1]], base=0, channel_multiplier=0, **fine).then_inc(const_ready, 1)
            g.iota(tile_no[:, :], pattern=[[1, NT]], base=0, channel_multiplier=0, **fine).then_inc(const_ready, 1)
            g.iota(part_no1[:, :], pattern=[[0, 1]], base=1, channel_multiplier=1, **fine).then_inc(const_ready, 1)
            g.memset(ones[:, :], 1.0).then_inc(const_ready, 1)
            g.memset(ones_f[:, :], 1.0).then_inc(const_ready, 1)
            g.memset(v_all[:, :, E + D:E + KVW], 1.0).then_inc(aug_ready, 1)
            for c in range(NCH):
                part = slice(c * TC, (c + 1) * TC)
                pool.wait_ge(zscale_ready, c + 1)
                pool.wait_ge(xn_by_dve, (c + 1) * TC // TG)
                pool.wait_ge(xn_by_act, (c + 1) * TC // TG)
                g.tensor_tensor(z[:, part, :], xn[:, part, :], zscale[:, part].unsqueeze(2).to_broadcast([P, TC, D]),
                                ALU.mult).then_inc(z_ready, 1)
                if c < NCH - 1:
                    add = g.tensor_tensor(base[:, part, :], x[:, part, :], xn[:, part, :], ALU.add)
            add.then_inc(base_ready, 1)

            def tile_values():
                pool.wait_ge(slot_hot_ready, 1)
                g.tensor_tensor(slot_val[:, :, 1, :], slot_hot[:, :, :], tile_no[:, :].unsqueeze(2).to_broadcast([P, NT, NSLOT]),
                                ALU.mult).then_inc(tile_val_ready, 1)

            def features_k(b, par):
                pool.wait_ge(k_exp_ready, b + 1)
                g.tensor_tensor(feat_k[:, TB * b:TB * (b + 1), :].rearrange("p j d -> p (j d)"), k_pos[:, par, :], k_exp[:, par, :],
                                ALU.add).then_inc(k_ready, 1)

            pool.wait_ge(base_ready, 1)
            pool.wait_ge(last_base_ready, 1)
            def gather(s):
                wait_for(pool, zt_done, s - RING + 1)
                g.indirect_dma_start(
                    out=rows[:, s % RING, :], out_offset=None, in_=z_dram,
                    in_offset=bass.IndirectOffsetOnAxis(ap=gather_at[:, s:s + 1], axis=0),
                ).then_inc(gather_in[s % AHEAD], 16)

            def landed(s):
                pool.wait_ge(gather_in[s % AHEAD], 16 * (s // AHEAD + 1))
                pool.sem_inc(gathered, 1)

            def scatter(s):
                pool.wait_ge(y_ready, s + 1)
                g.indirect_dma_start(
                    out=y_dram, out_offset=bass.IndirectOffsetOnAxis(ap=scatter_at[:, s:s + 1], axis=0),
                    in_=y_rows[:, s, :], in_offset=None, bounds_check=NTOK - 1, oob_is_err=False,
                ).then_inc(y_out, 16)

            for i in range(K_POOL):
                if i == TILE_AT:
                    tile_values()
                features_k(i, i % 2)

            pool.wait_ge(z_out, 16 * NCH)
            pool.wait_ge(index_ready, 1)
            sent = 0
            for s in range(NSLOT):
                if s >= AHEAD:
                    landed(s - AHEAD)
                gather(s)
                if s > RING and s % 3:
                    scatter(sent)
                    sent += 1
            for s in range(NSLOT - AHEAD, NSLOT):
                landed(s)
            pool.wait_ge(kv_copied, NB)
            g.tensor_tensor(kv_all[:, NB1:NB, :], kv_all[:, NB1:NB, :], head_mask[:, :].unsqueeze(1).to_broadcast([P, NB - NB1, KVW]),
                            ALU.mult).then_inc(last_kv_ready, 1)
            for s in range(sent, NSLOT):
                scatter(s)
            pool.wait_ge(base_ready, POOL_ADDS + 1)
            for b in range(POOL_ADDS):
                two = slice(TB * b, TB * (b + 1))
                pool.wait_ge(scaled, b + 1)
                g.tensor_tensor(base[:, two, :], base[:, two, :], y_back[:, two, :], ALU.add).then_inc(pool_added, 1)

        @block.scalar
        def _(act):
            a = nc.scalar

            def sqrt_of(c):
                act.wait_ge(var_ready, c + 1)
                a.activation(std[:, c, :, :], var_e[:, c, :, :], ACT.Sqrt).then_inc(std_ready, 1)

            def copy_xnT(gr):
                act.wait_ge(xt_done, gr + 1)
                a.activation(xnT[:, gr * TG * P:(gr + 1) * TG * P], bank[gr % 2][:, :], ACT.Copy).then_inc(xnT_ready, 1)

            def normalise(gr):
                c = gr * TG // TC
                act.wait_ge(rstd_ready, c + 1)
                for t in range(gr * TG, gr * TG + XN_ACT[c]):
                    last = a.activation(xn[:, t, :], x[:, t, :], ACT.Identity, bias=shift[:, t:t + 1],
                                        scale=rstd[:, c, 0, t % TC:t % TC + 1])
                last.then_inc(xn_by_act, 1)

            def copy_v(b):
                act.wait_ge(v_done, b + 1)
                a.activation(v_all[:, TB * b:TB * (b + 1), 0:E + D],
                             bank[2 + b % V_BANKS][:, 0:TB * (E + D)].rearrange("p (j d) -> p j d", j=TB), ACT.Copy).then_inc(v_copied, 1)

            sqrt_of(0)
            normalise(0)
            normalise(1)
            sqrt_of(1)
            for gr in range(NG + LAG):
                if gr < NG:
                    copy_xnT(gr)
                for j in range(TG // TB):
                    if gr >= LAG:
                        copy_v((gr - LAG) * TG // TB + j)
                    if j == 0 and gr % 2 and (gr + 3) // 2 < NCH:
                        sqrt_of((gr + 3) // 2)
                if gr + 2 < NG:
                    normalise(gr + 2)
            act.wait_ge(max_ready, 1)
            a.activation(alpha_e[:, :], aff_max[:, :], ACT.Exp, scale=-1.0).then_inc(sig_exp, 1)

            def exp_of_k(b, par):
                act.wait_ge(k_done, b + 1)
                a.activation(k_neg[:, par, :], bank[par][:, 0:TB * P], ACT.Relu, scale=-1.0).then_inc(k_neg_ready, 1)
                wait_batch(act, k_ready, k_by_dve, b - 2)
                if b < K_POOL:
                    a.activation(k_pos[:, par, :], bank[par][:, 0:TB * P], ACT.Relu).then_inc(k_read, 1)
                act.wait_ge(k_neg_ready, b + 1)
                a.activation(k_exp[:, par, :], k_neg[:, par, :], ACT.Exp, scale=-1.0).then_inc(k_exp_ready, 1)

            def copy_kv(b):
                act.wait_ge(kv_done, b + 1)
                a.activation(kv_all[:, b, :], bank[4 + b % KV_BANKS][:, 0:KVW], ACT.Copy).then_inc(kv_copied, 1)

            def part_values():
                act.wait_ge(slot_hot_ready, 1)
                a.activation(slot_val[:, :, 0, :], slot_hot[:, :, :], ACT.Identity, scale=part_no1[:, :]).then_inc(part_val_ready, 1)

            for i in range(NB + KV_LAG + 1):
                if i == PART_AT:
                    part_values()
                if i < NB:
                    exp_of_k(i, i % 2)
                if i > KV_LAG:
                    copy_kv(i - KV_LAG - 1)

            def exp_of_q(b, par, last=False):
                act.wait_ge(q_done, b + 1)
                a.activation(q_neg[:, par, :], bank_of(Q, par, last)[:, 0:TB * P], ACT.Relu, scale=-1.0).then_inc(q_neg_ready, 1)
                act.wait_ge(q_neg_ready, b + 1)
                a.activation(q_exp[:, par, :], q_neg[:, par, :], ACT.Exp, scale=-1.0).then_inc(q_exp_ready, 1)

            def copy_headsT(b, par, last=False):
                act.wait_ge(ht_done, b + 1)
                a.activation(headsT[:, par, :], bank_of(HT, par, last)[:, 0:TB * P], ACT.Copy).then_inc(ht_copied, 1)

            def hidden(s, par, e):
                act.wait_ge(h_done, s + 1)
                for c in range(FC):
                    last = a.activation(hT[:, par, c * P:(c + 1) * P], bank[2 + par][:, c * P:(c + 1) * P], ACT.Relu,
                                        bias=b1[:, c, bass.ds(e, 1)])
                last.then_inc(h_ready, 1)

            act.wait_ge(bias_in, 16 * 2)
            act.wait_ge(expert_ready, 2)
            first_experts = [act.value_load(ex_i[0:1, s:s + 1], min_val=0, max_val=E - 1) for s in (0, 1)]
            exp_of_q(0, 0)
            hidden(0, 0, first_experts[0])
            copy_headsT(0, 0)
            hidden(1, 1, first_experts[1])
            with act.Fori(0, TURNS) as k:
                for n in range(RING):
                    s, b, stage = k * RING + (n + 2), k * (RING // TPB) + (n // TPB + EARLY), n % TPB
                    if n % 2 == 0:
                        v = act.value_load(ex_pair[0:1, bass.ds(k * (RING // 2) + n // 2, 1)], min_val=0, max_val=E ** WORD - 1)
                    if stage == 0:
                        exp_of_q(b, 0)
                    if stage == 2:
                        copy_headsT(b, 0)
                    hidden(s, n % 2, slot(v, 2 + n % 2))
            hidden(NSLOT - 1, 0, act.value_load(ex_i[0:1, NSLOT - 1:NSLOT], min_val=0, max_val=E - 1))

            def scale_rows(b):
                act.wait_ge(y_in[b // YB], 16)
                for t in range(TB * b, TB * (b + 1)):
                    last = a.activation(y_back[:, t, :], y_back[:, t, :], ACT.Identity, scale=alpha[:, t:t + 1])
                last.then_inc(scaled, 1)

            act.wait_ge(alpha_ready, 1)
            for i in range(NB - NB1 + 2):
                if i < NB - NB1:
                    exp_of_q(NB1 + i, (NB1 + i) % 2, last=True)
                if i >= 2:
                    copy_headsT(NB1 + i - 2, (NB1 + i) % 2, last=True)
                for b in ACT_SCALES.get(i, ()):
                    scale_rows(b)

        @block.tensor
        def _(pe):
            t_ = nc.tensor
            pe.wait_ge(ident_ready, 1)

            def transpose_x(gr):
                pe.wait_ge(xn_by_dve, gr + 1)
                pe.wait_ge(xn_by_act, gr + 1)
                wait_for(pe, xnT_ready, gr - 1)
                for j in range(TG):
                    last = t_.transpose(bank[gr % 2][:, j * P:(j + 1) * P], xn[:, gr * TG + j, :], ident[:, :])
                last.then_inc(xt_done, 1)

            def values(b):
                pe.wait_ge(xnT_ready, TB * b // TG + 1)
                wait_for(pe, v_copied, b - V_BANKS + 1)
                for j in range(TB):
                    t = TB * b + j
                    last = t_.matmul(bank[2 + b % V_BANKS][:, j * (E + D):(j + 1) * (E + D)], xnT[:, t * P:(t + 1) * P], cent_wv[:, :],
                                     start=True, stop=True)
                last.then_inc(v_done, 1)

            for gr in range(NG):
                transpose_x(gr)
                if gr == LAG:
                    pe.wait_ge(cent_wv_in, 16 * 2)
                for b in range((gr - LAG) * TG // TB, (gr - LAG + 1) * TG // TB):
                    if b >= 0:
                        values(b)
            for b in range((NG - LAG) * TG // TB, NB):
                values(b)

            def project_k(b):
                wait_batch(pe, k_read, k_by_dve, b - 2)
                for j in range(TB):
                    t = TB * b + j
                    last = t_.matmul(bank[b % 2][:, j * P:(j + 1) * P], xnT[:, t * P:(t + 1) * P], wk[:, :], start=True, stop=True)
                last.then_inc(k_done, 1)

            def keys_values(b):
                wait_batch(pe, k_ready, k_by_dve, b)
                wait_for(pe, kv_copied, b - KV_BANKS + 1)
                for j in range(TB):
                    last = t_.matmul(bank[4 + b % KV_BANKS][:, 0:KVW], feat_k[:, TB * b + j, :], v_all[:, TB * b + j, E:E + KVW],
                                     start=(j == 0), stop=(j == TB - 1))
                last.then_inc(kv_done, 1)

            def ranks():
                pe.wait_ge(const_ready, 10)
                pe.wait_ge(chosen_ready, 1)
                hot = chosen[:, :, :].rearrange("p e t -> p (e t)")
                t_.matmul(bank[7][:, 0:E * NT], before[:, :], hot, start=True, stop=True)
                t_.matmul(bank[7][:, E * NT:2 * E * NT], ones[:, :], hot, start=True, stop=True).then_inc(ranks_done, 1)

            def tokens():
                pe.wait_ge(part_val_ready, 1)
                pe.wait_ge(tile_val_ready, 1)
                for t in range(NT):
                    if t % LANES_PIECE == 0:
                        pe.wait_ge(lane_ready, t // LANES_PIECE + 1)
                    last = t_.matmul(bank[7][:, 0:2 * NSLOT], lane_hot[:, t, :],
                                     slot_val[:, t, :, :].rearrange("p a s -> p (a s)"), start=(t == 0), stop=(t == NT - 1))
                last.then_inc(tok_done, 1)

            pe.wait_ge(attw_in, 16 * 3)
            pe.wait_ge(aug_ready, 1)
            pe.wait_ge(xnT_ready, NG)
            for i in range(NB + KV_LAG):
                if i == RANKS_AT:
                    pe.wait_ge(v_copied, NB)
                if i == RANKS_AT:
                    ranks()
                if i == TOKENS_AT:
                    tokens()
                if i < NB:
                    project_k(i)
                if i >= KV_LAG:
                    keys_values(i - KV_LAG)

            def project_q(b, par, last=False):
                t_.matmul(bank_of(Q, par, last)[:, 0:TB * P], wq[:, :], some(xnT, b * (TB * P), TB * P), start=True, stop=True)\
                  .then_inc(q_done, 1)

            def num(b, par, last=False):
                pe.wait_ge(q_ready, b + 1)
                if not last:
                    pe.wait_ge(base_ready, b + 1)
                if last:
                    pe.wait_ge(last_kv_ready, 1)
                if last and par == 0:
                    pe.wait_ge(base_ready, NB1 + 1)
                for j in range(TB):
                    mm = t_.matmul(bank_of(NUM, par, last)[:, j * KVW:(j + 1) * KVW], feat_q[:, par, j * P:(j + 1) * P],
                                   kv_all[:, b, :] if last else kv_m[:, par, :], start=True, stop=True)
                mm.then_inc(num_done, 1)

            def turn_heads(b, par, last=False):
                pe.wait_ge(heads_ready, b + 1)
                if last:
                    pe.wait_ge(ht_copied, b)
                for j in range(TB):
                    mm = t_.transpose(bank_of(HT, par, last)[:, j * P:(j + 1) * P], heads[:, j, :], ident[:, :])
                mm.then_inc(ht_done, 1)

            def out_project(b, par, last=False):
                pe.wait_ge(ht_copied, b + 1)
                if last:
                    pe.wait_ge(base_ready, b + 1)
                for j in range(TB):
                    mm = t_.matmul(bank_of(OUT, par, last)[:, j * D:(j + 1) * D], headsT[:, par, j * P:(j + 1) * P], wo[:, :],
                                   start=True, stop=True)
                mm.then_inc(att_done, 1)

            def turn_rows(s, par, place):
                pe.wait_ge(gathered, s + 1)
                t_.transpose(bank[par][:, 0:P], rows[:, place, :], ident[:, :]).then_inc(zt_done, 1)

            def hidden(s, par):
                pe.wait_ge(zt_ready, s + 1)
                pe.wait_ge(w1_ready, s + 1)
                for c in range(FC):
                    last = t_.matmul(bank[2 + par][:, c * P:(c + 1) * P], w1_now[:, par, c * P:(c + 1) * P], zT[:, par, :],
                                     start=True, stop=True)
                last.then_inc(h_done, 1)

            def second(s, par, e):
                pe.wait_ge(h_ready, s + 1)
                wait_for(pe, y_ready, s - 1)
                for c in range(FC):
                    last = t_.matmul(bank[6 + par][:, 0:D], hT[:, par, c * P:(c + 1) * P],
                                     w2[:, bass.ds(e * (FC * D) + c * D, D)], start=(c == 0), stop=(c == FC - 1))
                last.then_inc(y_done, 1)

            pe.wait_ge(k_by_dve, NB - K_POOL)
            pe.wait_ge(index_ready, 1)
            pe.wait_ge(w2_in, 16)
            pe.wait_ge(expert_ready, 2)

            def expert_of(s):
                return pe.value_load(ex_i[0:1, s:s + 1], min_val=0, max_val=E - 1)

            turn_rows(0, 0, 0)
            turn_rows(1, 1, 1)
            pe.wait_ge(kv_copied, NB)
            project_q(0, 0)
            first_expert = expert_of(0)
            hidden(0, 0)
            turn_rows(2, 0, 2)
            num(0, 0)
            hidden(1, 1)
            turn_heads(0, 0)
            second(0, 0, first_expert)
            out_project(0, 0)
            with pe.Fori(0, TURNS) as k:
                for n in range(RING):
                    s, par, place = k * RING + (n + 2), n % 2, (n + 2) % RING
                    b, stage, b_par = k * (RING // TPB) + (n // TPB + EARLY), n % TPB, 0
                    if par == 0:
                        v = pe.value_load(ex_pair[0:1, bass.ds(k * (RING // 2) + n // 2, 1)], min_val=0, max_val=E ** WORD - 1)
                    if stage < 2:
                        (project_q, num)[stage](b, b_par)
                    turn_rows(s + 1, 1 - par, (place + 1) % RING)
                    hidden(s, par)
                    if stage == 2:
                        turn_heads(b, b_par)
                    second(s - 1, 1 - par, slot(v, 1 + par))
                    if stage == 2:
                        out_project(b, b_par)
            hidden(NSLOT - 1, 0)
            second(NSLOT - 2, 1, expert_of(NSLOT - 2))
            second(NSLOT - 1, 0, expert_of(NSLOT - 1))

            for i in range(NB - NB1 + 3):
                b, par = NB1 + i, (NB1 + i) % 2
                if i < NB - NB1:
                    project_q(b, par, last=True)
                if i >= 3:
                    out_project(b - 3, 1 - par, last=True)
                if 1 <= i < NB - NB1 + 1:
                    num(b - 1, 1 - par, last=True)
                if 2 <= i < NB - NB1 + 2:
                    turn_heads(b - 2, par, last=True)

        @block.vector
        def _(dve):
            v_ = nc.vector

            def statistics(c):
                if c < NCH:
                    dve.wait_ge(x_in[c] if c else x_first_in, 16)
                    for j in range(TC):
                        if c == 0 and j == X_FIRST:
                            dve.wait_ge(x_in[c], 16)
                        ins = v_.bn_stats(stats[:, c % 2, j, :], x[:, c * TC + j, :])
                        if j == TC - 1:
                            ins.then_inc(stat_done, 1)
                        yield

            chained = [0]

            def step(ins, filling):
                chained[0] += 1
                ins.then_inc(chain, 1)
                next(filling, None)
                dve.wait_ge(chain, chained[0])

            def moments(c, filling):
                st = stats[:, c % 2, :, :]
                mean_c = mean[:, c * TC:(c + 1) * TC]
                var = ms_b[:, 1, :]
                dve.wait_ge(stat_done, c + 1)
                v_.tensor_tensor(ms_a[:, 0, :], st[:, :, 1], st[:, :, 4], ALU.add)
                v_.tensor_tensor(ms_a[:, 1, :], st[:, :, 1], st[:, :, 4], ALU.subtract)
                step(v_.tensor_tensor(ms_a[:, 2, :], st[:, :, 2], st[:, :, 5], ALU.add), filling)
                v_.tensor_scalar(mean_c, ms_a[:, 0, :], 0.5, None, ALU.mult)
                step(v_.scalar_tensor_tensor(ms_b[:, 0, :], ms_a[:, 1, :], 0.25, ms_a[:, 1, :], ALU.mult, ALU.mult), filling)
                step(v_.scalar_tensor_tensor(var, ms_a[:, 2, :], 1.0 / D, ms_b[:, 0, :], ALU.mult, ALU.add), filling)
                v_.tensor_scalar(var_e[:, c, 0, :], var, 1.0, EPS_LN, ALU.mult, ALU.add)
                v_.tensor_scalar(var_e[:, c, 1, :], var, 1.0 + EPS_LN, EPS_LN * EPS_LN, ALU.mult, ALU.add).then_inc(var_ready, 1)

            def rsqrts(c, filling):
                part = slice(c * TC, (c + 1) * TC)
                dve.wait_ge(std_ready, c + 1)
                dve.wait_ge(var_ready, c + 1)
                step(v_.reciprocal(rinv[:, :, :], std[:, c, :, :]), filling)
                step(v_.tensor_tensor(nw_a[:, :, :], rinv[:, :, :], rinv[:, :, :], ALU.mult), filling)
                step(v_.tensor_tensor(nw_b[:, :, :], nw_a[:, :, :], var_e[:, c, :, :], ALU.mult), filling)
                step(v_.tensor_scalar(nw_a[:, :, :], nw_b[:, :, :], -0.5, 1.5, ALU.mult, ALU.add), filling)
                step(v_.tensor_tensor(rstd[:, c, :, :], rinv[:, :, :], nw_a[:, :, :], ALU.mult), filling)
                v_.scalar_tensor_tensor(shift[:, part], mean[:, part], -1.0, rstd[:, c, 0, :], ALU.mult, ALU.mult)\
                  .then_inc(rstd_ready, 1)
                step(v_.tensor_tensor(nw_c[:, :], var_e[:, c, 0, :], rstd[:, c, 0, :], ALU.mult), filling)
                v_.tensor_tensor(zscale[:, part], nw_c[:, :], rstd[:, c, 1, :], ALU.mult).then_inc(zscale_ready, 1)

            def normalise(c):
                for j in range(TC):
                    if j % TG >= XN_ACT[c]:
                        t = c * TC + j
                        ins = v_.tensor_scalar(xn[:, t, :], x[:, t, :], mean[:, t:t + 1], rstd[:, c, 0, j:j + 1], ALU.subtract, ALU.mult)
                        if j % TG == TG - 1:
                            ins.then_inc(xn_by_dve, 1)
                        yield

            def finish(work):
                for _ in work:
                    pass

            finish(statistics(0))
            filling = statistics(1)
            moments(0, filling)
            for c in range(NCH):
                rsqrts(c, filling)
                finish(filling)
                filling = normalise(c)
                if c + 1 < NCH:
                    moments(c + 1, filling)
                finish(filling)
                filling = statistics(c + 2)
            dve.wait_ge(xn_by_act, NG)
            dve.wait_ge(xn_by_dve, NG)
            part = slice((NCH - 1) * TC, NCH * TC)
            v_.tensor_tensor(base[:, part, :], x[:, part, :], xn[:, part, :], ALU.add).then_inc(last_base_ready, 1)
            dve.wait_ge(last_base_ready, 1)

            steps = [0]

            def then(ins):
                steps[0] += 1
                ins.then_inc(route, 1)
                dve.wait_ge(route, steps[0])

            def per_e(v):
                return v.unsqueeze(2).to_broadcast([P, E, NT])

            def per_t(v):
                return v.unsqueeze(1).to_broadcast([P, E, NT])

            def t_e(v):
                return v.rearrange("p e t -> p t e")

            ahead = upto[:, 0:E * NT].rearrange("p (e t) -> p e t", e=E)
            rank_p = bank[7][:, 0:E * NT].rearrange("p (e t) -> p e t", e=E)

            aff = v_all[:, :, 0:E]

            def choose():
                dve.wait_ge(v_copied, NB)
                v_.tensor_reduce(aff_max[:, :], aff, AX.X, ALU.max).then_inc(max_ready, 1)
                dve.wait_ge(max_ready, 1)
                dve.wait_ge(const_ready, 10)
                then(v_.tensor_tensor(rt_a[:, :, :], aff.rearrange("p t e -> p e t"), per_t(aff_max[:, :]), ALU.is_equal))
                then(v_.tensor_tensor(rt_b[:, :, :], rt_a[:, :, :], rank_e[:, :, :], ALU.mult))
                then(v_.tensor_reduce(first[:, :], t_e(rt_b[:, :, :]), AX.X, ALU.max))
                v_.tensor_tensor(chosen[:, :, :], rank_e[:, :, :], per_t(first[:, :]), ALU.is_equal).then_inc(chosen_ready, 1)

            def count():
                dve.wait_ge(ranks_done, 1)
                total_p = bank[7][:, E * NT:2 * E * NT]
                then(v_.tensor_tensor_scan(upto[:, 1:], ones_f[:, :], total_p, 0.0, ALU.mult, ALU.add))
                v_.scalar_tensor_tensor(n_i[:, :], upto[:, NT::NT], float(P - 1), ahead[:, :, 0], ALU.add, ALU.subtract)
                then(v_.tensor_tensor(rt_b[:, :, :], ahead, rank_p, ALU.add))
                then(v_.tensor_scalar(cnt_i[:, :], n_i[:, :], 7, None, ALU.arith_shift_right))
                then(v_.tensor_copy(cnt[:, :], cnt_i[:, :]))
                then(v_.tensor_tensor_scan(last_t[:, :], ones_f[:, 0:E], cnt[:, :], 0.0, ALU.mult, ALU.add))
                then(v_.tensor_tensor(start_t[:, :], last_t[:, :], cnt[:, :], ALU.subtract))
                then(v_.scalar_tensor_tensor(off[:, :], start_t[:, :], float(P), ahead[:, :, 0], ALU.mult, ALU.subtract))

            def place():
                then(v_.tensor_tensor(rt_c[:, :, :], rt_b[:, :, :], per_e(off[:, :]), ALU.add))
                then(v_.tensor_tensor(rt_a[:, :, :], rt_c[:, :, :], chosen[:, :, :], ALU.mult))
                then(v_.tensor_reduce(pos[:, :], t_e(rt_a[:, :, :]), AX.X, ALU.add))
                then(v_.tensor_copy(pos_i[:, :], pos[:, :]))
                v_.tensor_scalar(hi_i[:, :], pos_i[:, :], 7, None, ALU.arith_shift_right)
                then(v_.tensor_scalar(lo_i[:, :], pos_i[:, :], P - 1, None, ALU.bitwise_and))
                v_.tensor_copy(lo_f[:, :], lo_i[:, :])
                then(v_.tensor_copy(hi_f[:, :], hi_i[:, :]))

            def hot_lanes():
                for t in range(NT):
                    ins = v_.tensor_scalar(lane_hot[:, t, :], lane[:, :], lo_f[:, t:t + 1], None, ALU.is_equal)
                    if t % LANES_PIECE == LANES_PIECE - 1:
                        ins.then_inc(lane_ready, 1)

            def hot_slots():
                v_.tensor_tensor(slot_hot[:, :, :], slot_no[:, 0:NSLOT].unsqueeze(1).to_broadcast([P, NT, NSLOT]),
                                 hi_f[:, :].unsqueeze(2).to_broadcast([P, NT, NSLOT]), ALU.is_equal).then_inc(slot_hot_ready, 1)

            def weights():
                dve.wait_ge(sig_exp, 1)
                then(v_.tensor_scalar(alpha_1[:, :], alpha_e[:, :], 1.0, None, ALU.add))
                v_.reciprocal(alpha[:, :], alpha_1[:, :]).then_inc(alpha_ready, 1)

            def experts_of_tiles():
                then(v_.tensor_tensor(ex_cmp[:, :, :], slot_no[0:1, :].unsqueeze(2).to_broadcast([1, NSLOT + 1, E]),
                                      last_t[0:1, :].unsqueeze(1).to_broadcast([1, NSLOT + 1, E]), ALU.is_ge))
                then(v_.tensor_reduce(ex_f[:, :], ex_cmp[:, :, :], AX.X, ALU.add))

            def expert_words():
                then(v_.tensor_scalar(ex_m[:, :], ex_f[:, :], float(E - 1), None, ALU.min))
                v_.tensor_copy(ex_i[:, :], ex_m[:, :]).then_inc(expert_ready, 1)
                ev = [ex_m[:, j:j + 2 * PAIRS - 1:2] for j in range(WORD)]
                word = ev[WORD - 1]
                for j in reversed(range(1, WORD - 1)):
                    then(v_.scalar_tensor_tensor(ex_p[j % 2][:, :], word, float(E), ev[j], ALU.mult, ALU.add))
                    word = ex_p[j % 2][:, :]
                v_.scalar_tensor_tensor(ex_pair[:, :], word, float(E), ev[0], ALU.mult, ALU.add).then_inc(expert_ready, 1)

            def slot_tokens():
                dve.wait_ge(tok_done, 1)
                then(v_.tensor_copy(tok_c[:, :, :], bank[7][:, 0:2 * NSLOT].rearrange("p (a s) -> p a s", a=2)))
                then(v_.scalar_tensor_tensor(tok_f[:, :], tok_c[:, 1, :], float(P), tok_c[:, 0, :], ALU.mult, ALU.add))
                v_.tensor_scalar(gather_at[:, :], tok_f[:, :], -1.0, 0.0, ALU.add, ALU.max)
                then(v_.tensor_scalar(tok_neg[:, :], tok_f[:, :], 0.5, float(2 * NTOK), ALU.is_lt, ALU.mult))
                v_.scalar_tensor_tensor(scatter_at[:, :], tok_f[:, :], -1.0, tok_neg[:, :], ALU.add, ALU.add).then_inc(index_ready, 1)

            def mask_kv(b, par):
                v_.tensor_tensor(kv_m[:, par, :], some(kv_all, b, 1).rearrange("p b c -> p (b c)"), head_mask[:, :], ALU.mult)

            def features_q(b, par, last=False):
                dve.wait_ge(q_exp_ready, b + 1)
                v_.scalar_tensor_tensor(feat_q[:, par, :], bank_of(Q, par, last)[:, 0:TB * P], 0.0, q_exp[:, par, :], ALU.max, ALU.add)\
                  .then_inc(q_ready, 1)

            def divide(b, par, last=False, between=None):
                dve.wait_ge(num_done, b + 1)
                nd = bank_of(NUM, par, last)[:, 0:TB * KVW].rearrange("p (j c) -> p j c", j=TB)
                v_.tensor_scalar(den[:, :, :], nd[:, :, D:KVW], EPS_ATT, None, ALU.add).then_inc(den_ready, 1)
                if between:
                    between()
                dve.wait_ge(den_ready, b + 1)
                v_.reciprocal(rden[:, :, :], den[:, :, :]).then_inc(rden_ready, 1)
                dve.wait_ge(rden_ready, b + 1)
                if last:
                    dve.wait_ge(ht_done, b)
                for j in range(TB):
                    ins = v_.tensor_tensor(heads[:, j, :].rearrange("p (h m) -> p h m", h=H),
                                            nd[:, j, 0:D].rearrange("p (h m) -> p h m", h=H),
                                            rden[:, j, :].unsqueeze(2).to_broadcast([P, H, HD]), ALU.mult)
                ins.then_inc(heads_ready, 1)

            def add_attention(b, par, last=False):
                dve.wait_ge(att_done, b + 1)
                two = some(base, b * TB, TB)
                v_.tensor_tensor(two, bank_of(OUT, par, last)[:, 0:TB * D].rearrange("p (j d) -> p j d", j=TB), two, ALU.add).then_inc(base_ready, 1)

            def turned(s, par, e):
                dve.wait_ge(zt_done, s + 1)
                wait_for(dve, h_done, s - 1)
                v_.tensor_scalar(zT[:, par, :], bank[par][:, 0:P], ln_g[:, bass.ds(e, 1)], ln_b[:, bass.ds(e, 1)],
                                 ALU.mult, ALU.add).then_inc(zt_ready, 1)
                v_.tensor_copy(w1_now[:, par, :], w1[:, bass.ds(e * F, F)]).then_inc(w1_ready, 1)

            def result(s, par, e):
                dve.wait_ge(y_done, s + 1)
                v_.tensor_tensor(some(y_rows, s, 1).rearrange("p s d -> p (s d)"), bank[6 + par][:, 0:D], b2[:, bass.ds(e * D, D)], ALU.add).then_inc(y_ready, 1)

            def expert_of(s):
                return dve.value_load(ex_i[0:1, s:s + 1], min_val=0, max_val=E - 1)

            def features_k(b):
                dve.wait_ge(k_exp_ready, b + 1)
                v_.scalar_tensor_tensor(feat_k[:, TB * b:TB * (b + 1), :].rearrange("p j d -> p (j d)"), bank[b % 2][:, 0:TB * P], 0.0,
                                        k_exp[:, b % 2, :], ALU.max, ALU.add).then_inc(k_by_dve, 1)

            for piece in (choose, count, place, hot_slots, hot_lanes, experts_of_tiles, slot_tokens, expert_words):
                piece()
            dve.wait_ge(expert_ready, 2)
            first_experts = []
            for b in range(K_POOL, NB):
                features_k(b)
                if b - K_POOL < 3:
                    first_experts.append(expert_of(b - K_POOL))

            dve.wait_ge(small_in, 16 * 2)
            dve.wait_ge(bias_in, 16 * 2)
            dve.wait_ge(w1_in, 16)
            turned(0, 0, first_experts[0])
            turned(1, 1, first_experts[1])
            dve.wait_ge(kv_copied, NB)
            mask_kv(0, 0)
            features_q(0, 0)
            turned(2, 0, first_experts[2])
            divide(0, 0)
            weights()
            add_attention(0, 0)
            with dve.Fori(0, TURNS) as k:
                for n in range(RING):
                    s, b, stage = k * RING + (n + 2), k * (RING // TPB) + (n // TPB + EARLY), n % TPB
                    if n % 2 == 0:
                        v = dve.value_load(ex_pair[0:1, bass.ds(k * (RING // 2) + n // 2, 1)], min_val=0, max_val=E ** WORD - 1)
                    if stage == 0:
                        mask_kv(b, 0)
                    result(s - 2, n % 2, slot(v, n % 2))
                    if stage == 0:
                        features_q(b, 0)
                    turned(s + 1, 1 - n % 2, slot(v, n % 2 + 3))
                    if stage in (1, 2):
                        (divide, add_attention)[stage - 1](b, 0)
            for s in range(NSLOT - 3, NSLOT):
                result(s, s % 2, expert_of(s))

            def add_experts(b):
                dve.wait_ge(y_in[b // YB], 16)
                dve.wait_ge(base_ready, b + 2)
                for t in range(TB * b, TB * (b + 1)):
                    last = v_.scalar_tensor_tensor(base[:, t, :], y_back[:, t, :], alpha[:, t:t + 1], base[:, t, :], ALU.mult, ALU.add)
                last.then_inc(dve_added, 1)

            for i in range(NB - NB1 + 3):
                b, par = NB1 + i, (NB1 + i) % 2
                if i < NB - NB1:
                    features_q(b, par, last=True)
                add = (lambda: add_attention(b - 3, 1 - par, last=True)) if i >= 3 else None
                if 1 <= i < NB - NB1 + 1:
                    divide(b - 1, 1 - par, last=True, between=add)
                elif add:
                    add()
                for b in DVE_ADDS.get(i, ()):
                    add_experts(b)


def kernel(L0_attn_x, L0_attn_Wq, L0_attn_Wk, L0_attn_Wv, L0_attn_Wo, L0_ffn_centroids, L0_ffn_ln_g, L0_ffn_ln_b,
           L0_ffn_w1, L0_ffn_b1, L0_ffn_w2, L0_ffn_b2):
    import numpy as np
    import concourse.bacc as bacc
    from concourse.bass_utils import run_bass_kernel_spmd

    P = 128
    x = np.ascontiguousarray(L0_attn_x)
    w1, b1, w2 = (np.asarray(v) for v in (L0_ffn_w1, L0_ffn_b1, L0_ffn_w2))
    E, F, D = w1.shape
    C = F // P
    laid = {
        "x": x,
        "wqT": np.asarray(L0_attn_Wq).T, "wkT": np.asarray(L0_attn_Wk).T,
        "wvT": np.asarray(L0_attn_Wv).T, "woT": np.asarray(L0_attn_Wo).T,
        "centT": np.asarray(L0_ffn_centroids).T, "gT": np.asarray(L0_ffn_ln_g).T, "bT": np.asarray(L0_ffn_ln_b).T,
        "w1T": w1.transpose(2, 0, 1).reshape(D, E * F),
        "b1T": b1.reshape(E, C, P).transpose(2, 1, 0),
        "w2T": w2.reshape(E, D, C, P).transpose(3, 0, 2, 1).reshape(P, E * C * D),
        "b2": np.asarray(L0_ffn_b2),
    }
    nc = bacc.Bacc("TRN2", target_bir_lowering=False, num_devices=1)
    arrays, args = {}, []
    for name, a in laid.items():
        a = np.ascontiguousarray(a)
        arrays["in_" + name] = a
        args.append(nc.dram_tensor("in_" + name, a.shape, mybir.dt.from_np(a.dtype), kind="ExternalInput").ap())
    args.append(nc.dram_tensor("out", x.shape, mybir.dt.from_np(x.dtype), kind="ExternalOutput").ap())
    linear_attention_and_routed_experts(nc, *args)
    r = run_bass_kernel_spmd(nc, [arrays], core_ids=[0])
    return r.results[0]["out"]
```
